# Optimizing a Trainium2 kernel written in Bass

```python
import numpy as np
import jax
import jax.numpy as jnp

def _softmax(x, axis=-1):
    return jax.nn.softmax(x, axis=axis)

def _gelu(x):
    return jax.nn.gelu(x, approximate=True)

def _silu(x):
    return jax.nn.silu(x)

def _sigmoid(x):
    return jax.nn.sigmoid(x)

def _layernorm(x, axis=-1, eps=1e-05):
    m = jnp.mean(x, axis=axis, keepdims=True)
    v = jnp.var(x, axis=axis, keepdims=True)
    return (x - m) / jnp.sqrt(v + eps)

def _scatter_add(tgt, idx, src, axis=0):
    return tgt.at[idx].add(src)

def _segment_sum(src, seg, n):
    return jax.ops.segment_sum(src, seg, n)
kernel_name = 'mk_adj_resnorm_d4_adj_r2_156093'

def setup_inputs(seed: int=0):
    np.random.seed(seed)
    _w = jnp.asarray

    def _rec_inputs():
        import jax
        import jax.numpy as jnp
        _gk = jax.random.key(seed)
        x = -9.806e-05 + 1 * jax.random.normal(jax.random.fold_in(_gk, 1), (4096, 128), jnp.float32)
        _a = jax.random.bernoulli(jax.random.fold_in(_gk, 2), 0.000488281, (4096, 4096))
        _a = jnp.logical_or(_a, jnp.eye(4096, dtype=bool))
        _af = _a.astype(jnp.float32)
        _af = _af * jax.random.uniform(jax.random.fold_in(_gk, 3), (4096, 4096), jnp.float32, 0.05, 1)
        adj = _af
        return (x, adj)
    x, adj = _rec_inputs()

    def _L0_gnn_setup():
        import jax, jax.numpy as jnp
        import numpy as np

        def _lap_mul(A, x):
            d = 1.0 / jnp.sqrt(jnp.sum(A, axis=-1))
            return d[:, None] * (A @ (d[:, None] * x))
        key = jax.random.key(seed)
        k1, k2, k3, k4, k5, k6 = jax.random.split(key, 6)
        N, D_IN, D_OUT = (2048, 128, 128)
        x = jax.random.normal(k1, (N, D_IN), dtype=jnp.float32)
        A = jax.random.uniform(k2, (N, N), dtype=jnp.float32)
        s1 = 1.0 / np.sqrt(D_IN)
        W1 = jax.random.uniform(k3, (D_IN, D_OUT), minval=-s1, maxval=s1, dtype=jnp.float32)
        b1 = jax.random.uniform(k4, (D_OUT,), minval=-s1, maxval=s1, dtype=jnp.float32)
        W2 = jax.random.uniform(k5, (D_IN, D_OUT), minval=-s1, maxval=s1, dtype=jnp.float32)
        b2 = jax.random.uniform(k6, (D_OUT,), minval=-s1, maxval=s1, dtype=jnp.float32)
        return {'x': x, 'A': A, 'W1': W1, 'b1': b1, 'W2': W2, 'b2': b2, 'sigma': 1, 'k': 4}
    _L0_gnn_all = _L0_gnn_setup()
    _L0_gnn_in = {k: v for k, v in _L0_gnn_all.items() if k in ('W1', 'b1', 'W2', 'b2')}
    del _L0_gnn_all

    def _L1_gnn_setup():
        import jax, jax.numpy as jnp
        import numpy as np
        N = 4096
        D = 128
        key = jax.random.key(seed)
        kx, ka, kw1, kw2 = jax.random.split(key, 4)
        x = jax.random.normal(kx, (N, D), dtype=jnp.float32)
        A = jax.random.uniform(ka, (N, N), dtype=jnp.float32)
        s = 0.05
        W1 = jax.random.normal(kw1, (D, D), dtype=jnp.float32) * s
        b1 = jnp.zeros((D,), dtype=jnp.float32)
        W2 = jax.random.normal(kw2, (D, D), dtype=jnp.float32) * s
        b2 = jnp.zeros((D,), dtype=jnp.float32)
        return {'x': x, 'A': A, 'W1': W1, 'b1': b1, 'W2': W2, 'b2': b2}
    _L1_gnn_all = _L1_gnn_setup()
    _L1_gnn_in = {k: v for k, v in _L1_gnn_all.items() if k in ('W1', 'b1', 'W2', 'b2')}
    del _L1_gnn_all

    def _L2_gnn_setup():
        import jax, jax.numpy as jnp
        import numpy as np
        EPS = 1e-05
        MIN_NORM = 1e-15

        def _norm(x):
            return jnp.maximum(jnp.linalg.norm(x, axis=-1, keepdims=True), MIN_NORM)

        def _artanh(x):
            return jnp.arctanh(jnp.clip(x, -1.0 + EPS, 1.0 - EPS))

        def expmap0(u):
            un = _norm(u)
            return jnp.tanh(un) * u / un

        def logmap0(y):
            yn = _norm(y)
            return _artanh(yn) * y / yn

        def mobius_matvec(W, x):
            mx = x @ W
            xn = _norm(x)
            mxn = _norm(mx)
            res = jnp.tanh(mxn / xn * _artanh(xn)) * mx / mxn
            zero = jnp.all(mx == 0.0, axis=-1, keepdims=True)
            return jnp.where(zero, 0.0, res)

        def mobius_scalar_mul(r, x):
            xn = _norm(x)
            return jnp.tanh(r * _artanh(xn)) * x / xn

        def _clamp_abs(x, eps=1e-10):
            return jnp.where(x >= 0.0, jnp.maximum(x, eps), jnp.minimum(x, -eps))
        key = jax.random.key(seed)
        k1, k2, k3 = jax.random.split(key, 3)
        N, D_IN, D_OUT = (4096, 128, 128)
        AVG_DEG = 64.0
        v = 0.1 * jax.random.normal(k1, (N, D_IN), dtype=jnp.float32)
        X = expmap0(v)
        mask = (jax.random.uniform(k2, (N, N)) < AVG_DEG / N).astype(jnp.float32)
        mask = mask + jnp.eye(N, dtype=jnp.float32)
        A_hat = mask / mask.sum(-1, keepdims=True)
        W = jax.random.uniform(k3, (D_IN, D_OUT), dtype=jnp.float32)
        return {'X': X, 'A_hat': A_hat, 'W': W}
    _L2_gnn_all = _L2_gnn_setup()
    _L2_gnn_in = {k: v for k, v in _L2_gnn_all.items() if k in ('W',)}
    del _L2_gnn_all

    def _L3_gnn_setup():
        import jax, jax.numpy as jnp
        import numpy as np
        EPS = 1e-06
        key = jax.random.key(seed)
        k1, k2, k3 = jax.random.split(key, 3)
        N, F_IN, F_OUT = (4096, 128, 128)
        x = jax.random.normal(k1, (N, F_IN), dtype=jnp.float32)
        adj = jax.random.uniform(k2, (N, N), dtype=jnp.float32)
        stdv = 1.0 / np.sqrt(F_OUT)
        weight = jax.random.uniform(k3, (F_IN, F_OUT), dtype=jnp.float32, minval=-stdv, maxval=stdv)
        return {'x': x, 'adj': adj, 'weight': weight}
    _L3_gnn_all = _L3_gnn_setup()
    _L3_gnn_in = {k: v for k, v in _L3_gnn_all.items() if k in ('weight',)}
    del _L3_gnn_all
    return {'x': x, 'adj': adj, 'L0_gnn_W1': _L0_gnn_in['W1'], 'L0_gnn_b1': _L0_gnn_in['b1'], 'L0_gnn_W2': _L0_gnn_in['W2'], 'L0_gnn_b2': _L0_gnn_in['b2'], 'L1_gnn_W1': _L1_gnn_in['W1'], 'L1_gnn_b1': _L1_gnn_in['b1'], 'L1_gnn_W2': _L1_gnn_in['W2'], 'L1_gnn_b2': _L1_gnn_in['b2'], 'L2_gnn_W': _L2_gnn_in['W'], 'L3_gnn_weight': _L3_gnn_in['weight']}

def reference(x, adj, L0_gnn_W1, L0_gnn_b1, L0_gnn_W2, L0_gnn_b2, L1_gnn_W1, L1_gnn_b1, L1_gnn_W2, L1_gnn_b2, L2_gnn_W, L3_gnn_weight):
    import jax
    import jax.numpy as jnp

    def _L0_gnn_ref(x, A, W1, b1, W2, b2, sigma, k):
        import jax, jax.numpy as jnp
        import numpy as np

        def _lap_mul(A, x):
            d = 1.0 / jnp.sqrt(jnp.sum(A, axis=-1))
            return d[:, None] * (A @ (d[:, None] * x))
        z = _lap_mul(A, x) @ W1 + b1
        z = jax.nn.leaky_relu(z, negative_slope=0.1)
        sq = jnp.sum(z * z, axis=-1)
        d2 = sq[:, None] + sq[None, :] - 2.0 * (z @ z.T)
        d2 = jnp.maximum(d2, 0.0)
        S = jnp.sqrt(d2 + 1e-10)
        S = jnp.exp(-S / (2.0 * sigma))
        order = jnp.argsort(-S, axis=-1)
        ranks = jnp.argsort(order, axis=-1)
        S = jnp.where(ranks < k, S, 0.0)
        A2 = S + A
        out = _lap_mul(A2, x) @ W2 + b2
        return out

    def _L1_gnn_ref(x, A, W1, b1, W2, b2):
        import jax, jax.numpy as jnp
        import numpy as np
        N = 4096
        D = 128
        h = jax.nn.relu(jnp.matmul(A, jnp.matmul(x, W1)) + b1)
        h = jax.nn.relu(jnp.matmul(A, jnp.matmul(h, W2)) + b2)
        return h

    def _L2_gnn_ref(X, A_hat, W):
        import jax, jax.numpy as jnp
        import numpy as np
        EPS = 1e-05
        MIN_NORM = 1e-15

        def _norm(x):
            return jnp.maximum(jnp.linalg.norm(x, axis=-1, keepdims=True), MIN_NORM)

        def _artanh(x):
            return jnp.arctanh(jnp.clip(x, -1.0 + EPS, 1.0 - EPS))

        def expmap0(u):
            un = _norm(u)
            return jnp.tanh(un) * u / un

        def logmap0(y):
            yn = _norm(y)
            return _artanh(yn) * y / yn

        def mobius_matvec(W, x):
            mx = x @ W
            xn = _norm(x)
            mxn = _norm(mx)
            res = jnp.tanh(mxn / xn * _artanh(xn)) * mx / mxn
            zero = jnp.all(mx == 0.0, axis=-1, keepdims=True)
            return jnp.where(zero, 0.0, res)

        def mobius_scalar_mul(r, x):
            xn = _norm(x)
            return jnp.tanh(r * _artanh(xn)) * x / xn

        def _clamp_abs(x, eps=1e-10):
            return jnp.where(x >= 0.0, jnp.maximum(x, eps), jnp.minimum(x, -eps))
        XW = mobius_matvec(W, X)
        sq = jnp.sum(XW * XW, axis=-1, keepdims=True)
        gamma = 2.0 / jnp.maximum(1.0 - sq, EPS)
        nominator = A_hat @ (gamma * XW)
        denominator = _clamp_abs(A_hat @ (gamma - 1.0))
        two_mean = nominator / denominator
        m = mobius_scalar_mul(0.5, two_mean)
        r = A_hat.sum(-1, keepdims=True)
        AXW = mobius_scalar_mul(r, m)
        return expmap0(jax.nn.relu(logmap0(AXW)))

    def _L3_gnn_ref(x, adj, weight):
        import jax, jax.numpy as jnp
        import numpy as np
        EPS = 1e-06
        N = adj.shape[0]
        a_tilde = adj + jnp.eye(N, dtype=adj.dtype)
        d_inv_sqrt = jax.lax.rsqrt(jnp.sum(adj, axis=1) + EPS)
        adj_norm = d_inv_sqrt[:, None] * a_tilde * d_inv_sqrt[None, :]
        support = x @ weight
        return adj_norm @ support
    x = _layernorm(x + _L0_gnn_ref(x, adj, L0_gnn_W1, L0_gnn_b1, L0_gnn_W2, L0_gnn_b2, 1, 4), axis=-1)
    x = _layernorm(x + _L1_gnn_ref(x, adj, L1_gnn_W1, L1_gnn_b1, L1_gnn_W2, L1_gnn_b2), axis=-1)
    x = _layernorm(x + _L2_gnn_ref(x, adj, L2_gnn_W), axis=-1)
    x = _layernorm(x + _L3_gnn_ref(x, adj, L3_gnn_weight), axis=-1)
    return x

_drawn_inputs = setup_inputs


def setup_inputs(seed=0):
    import zlib

    import numpy as np

    out = dict(_drawn_inputs(seed))
    spreads = {'L1_gnn_b1': (0.0, 0.1), 'L1_gnn_b2': (0.0, 0.1)}
    factors = {}
    for name, (base, spread) in spreads.items():
        noise = np.random.default_rng([zlib.crc32(name.encode()), seed]).standard_normal(out[name].shape)
        drawn = base * np.exp(spread * noise) if base else spread * noise
        out[name] = jnp.asarray(drawn.astype(out[name].dtype))
    for name, factor in factors.items():
        out[name] = (out[name] * factor).astype(out[name].dtype)
    return out
```

```python
import concourse.bass as bass
from concourse import mybir
from concourse.alu_op_type import AluOpType as ALU
from contextlib import ExitStack

F32 = mybir.dt.float32
F32R = mybir.dt.float32r
U32 = mybir.dt.uint32
ACT = mybir.ActivationFunctionType
AX = mybir.AxisListType

N, D, P = 4096, 128, 128
PANELS = 4
PW = N // PANELS
KT = PW // P
PIECES = 16
JT = N // P // PIECES
BANK = 512
CH = PW // BANK
RAW = 8
HI = 4
LN_EPS, L3_EPS, TOP = 1e-5, 1e-6, 4
CLIP, MIN_NORM, TINY = 1.0 - 1e-5, 1e-15, 1e-10

SUMS, SMOOTH, KNN, GCN1, GCN2, HYPER, NORMED = range(7)
BUF = {SMOOTH: 0, KNN: 0, GCN1: 1, GCN2: 0, HYPER: 1, NORMED: 0}
ZBUF = 1
POOL_Q = {SMOOTH: (3, 7, 11, 15), KNN: (), GCN1: (3, 7, 11, 15), GCN2: (3, 7, 11, 15),
          HYPER: (0, 2, 4, 6, 8, 10, 12, 14), NORMED: (3, 7, 11, 15)}
STREAMED = range(SMOOTH, NORMED + 1)
NEAR = -1


def build(nc, at, x, w01, b01, w02, b02, w11, b11, w12, b12, w2, w3, out):
    x_dram = {SUMS: x, NEAR: x, KNN: x, GCN2: nc.dram_tensor("x_after_0", [PANELS, P, KT * D], F32).ap(),
              HYPER: nc.dram_tensor("x_after_1", [PANELS, P, KT * D], F32).ap(),
              NORMED: nc.dram_tensor("x_after_2", [PANELS, P, KT * D], F32).ap()}
    scaled_rows = nc.dram_tensor("scaled_rows", [N, D], F32).ap()

    ctx = ExitStack()
    with ctx:
        def sem(name):
            return ctx.enter_context(nc.semaphore(name))

        arena_bytes = 211968
        ctx.enter_context(nc.sbuf_tensor("arena", [P, arena_bytes // 4], F32))
        base = nc.sbuf_base - arena_bytes
        top = [base]

        def at_byte(name, shape, dtype, offset):
            return nc.alloc_sbuf_tensor_at(name, [P, *shape], dtype, offset=offset)

        def place(name, shape, dtype):
            size = 4
            for s in shape:
                size *= s
            offset = top[0]
            top[0] += (size + 31) // 32 * 32
            assert top[0] <= base + arena_bytes, name
            return at_byte(name, shape, dtype, offset), offset

        raw, raw_at = place("raw", [RAW, JT, PW], F32)
        low = at_byte("low", [RAW, JT, PW], F32R, raw_at)
        high, high_at = place("high", [HI, JT, PW], F32R)
        scores = [at_byte(f"scores{i}", [N], F32, high_at + i * 4 * N) for i in range(2)]
        xh = [place(f"xh{i}", [N // P, D], F32R)[0] for i in range(2)]
        xl = [place(f"xl{i}", [N // P, D], F32R)[0] for i in range(2)]
        zh = xh[ZBUF][:, :, :].rearrange("p t d -> p (t d)")
        zl = xl[ZBUF][:, :, :].rearrange("p t d -> p (t d)")
        d_bc, d_at = place("d_bc", [N], F32)
        h_rows = at_byte("h_rows", [N], F32R, d_at)
        gathered = at_byte("gathered", [KT, TOP, D], F32, d_at)
        g_sum = at_byte("g_sum", [PW], F32, d_at)
        g_whole = at_byte("g_whole", [PW], F32, d_at + 4 * PW)
        t0, t0_at = place("t0", [PW], F32)
        t1, _ = place("t1", [PW], F32)
        t2, _ = place("t2", [PW], F32)
        a_sum = at_byte("a_sum", [JT, PW], F32, t0_at)
        xr, _ = place("xr", [PW], F32)
        w_names = ("w01", "w02", "w11", "w12", "w2", "w3")
        w = {n: place(n + "_sb", [D], F32)[0] for n in w_names}
        b02_bc, _ = place("b02_bc", [D], F32)
        b_cols, _ = place("b_cols", [3], F32)
        ident, _ = place("ident", [P], F32)
        ones, _ = place("ones", [P], F32)
        neg_half, _ = place("neg_half", [P], F32)
        ones_r, _ = place("ones_r", [P], F32R)
        z_tile_h = [place(f"z_tile_h{i}", [P], F32R)[0] for i in range(2)]
        z_tile_l = [place(f"z_tile_l{i}", [P], F32R)[0] for i in range(2)]
        top_v, _ = place("top_v", [KT, 8], F32)
        top_i, _ = place("top_i", [KT, 8], U32)
        near_i, _ = place("near_i", [N // P, TOP], U32)
        near_s, _ = place("near_s", [N // P, TOP], F32)
        ids, _ = place("ids", [KT, TOP], U32)
        dist, _ = place("dist", [KT, TOP], F32)
        a_rows, _ = place("a_rows", [N // P], F32)
        d_col, _ = place("d_col", [N // P], F32)
        s_col, _ = place("s_col", [N // P], F32)
        d2_col, _ = place("d2_col", [N // P], F32)
        sq_col, _ = place("sq_col", [N // P], F32)
        g_col, _ = place("g_col", [N // P], F32)
        stats, _ = place("stats", [KT, 6], F32)
        mv, _ = place("mv", [KT, 2], F32)
        c, _ = place("c", [16, KT], F32)

        ps = ctx.enter_context(nc.psum_tensor("ps", [P, 8 * BANK], F32))
        E0, E1 = 4 * BANK, 6 * BANK
        e0, e1 = ps[:, E0:E0 + PW], ps[:, E1:E1 + PW]

        def acc(p, lo=0, n=PW):
            return ps[:, bass.ds(p % 2 * PW + lo, n)]

        def part(t, p, n=PW):
            return t[:, bass.ds(p * n, n)]

        def rows(t):
            return t.rearrange("p (t d) -> p t d", d=D)

        def tiles(t, p):
            return t[:, bass.ds(p * KT, KT), :]

        def bc(t, n=D):
            return t.unsqueeze(2).to_broadcast([P, KT, n])

        loaded = [sem(f"loaded{i}") for i in range(RAW)]
        raw_free = sem("raw_free")
        hi_ready, lo_dve, lo_pool = sem("hi_ready"), sem("lo_dve"), sem("lo_pool")
        acc_free = sem("acc_free")
        consts_in, consts_up = sem("consts_in"), sem("consts_up")
        xr_in, xr_used = sem("xr_in"), sem("xr_used")
        stored = sem("stored")
        act_step = sem("act_step")
        S = {}

        def flag(name):
            if name not in S:
                S[name] = sem(name)
            return S[name]

        x_ready = {s: sem(f"x_ready{s}") for s in STREAMED}
        gathers = [sem(f"gathers{k}") for k in range(KT)]
        g_used = sem("g_used")
        x_stored = {s: sem(f"x_stored{s}") for s in (KNN, GCN2, HYPER, NORMED)}
        rows_stored = sem("rows_stored")

        def wait_apart(eng, which, value):
            eng.wait_ge(which, value)
            eng.sem_inc(flag("waited"), 1)

        class Chain:

            def __init__(self, eng, name, per):
                self.eng, self.sem, self.per = eng, flag(name), per

            def begin(self, p):
                self.p, self.k = p, 0

            def link(self, *ins, apart=False):
                for i in ins:
                    self.k += 1
                    i.then_inc(self.sem, 1)
                if apart:
                    wait_apart(self.eng, self.sem, self.per * self.p + self.k)
                else:
                    self.eng.wait_ge(self.sem, self.per * self.p + self.k)

            def end(self):
                assert self.k == self.per, (self.k, self.per)

        def piece(s, p, q):
            return 16 * (4 * (s - SMOOTH) + p) + q

        def consumed(s, p, q):
            return RAW + PANELS * PIECES + piece(s, p, q) + 1

        def slot_use(s, p, q):
            return 16 * (2 * (4 * s + p) + q // RAW + 1)

        def low_count(s, p, q):
            mine = q in POOL_Q[s]
            n = sum(PANELS * (len(POOL_Q[r]) if mine else PIECES - len(POOL_Q[r])) for r in range(SMOOTH, s))
            each = len(POOL_Q[s]) if mine else PIECES - len(POOL_Q[s])
            rank = sum((r in POOL_Q[s]) == mine for r in range(q + 1))
            return mine, n + each * p + rank

        def evictions(s, p):
            return 2 + 4 * (s - SMOOTH) + p + 1


        XR_USERS = (SUMS, NEAR, KNN, GCN2, HYPER, NORMED)

        def xr_count(user, p):
            return 4 * XR_USERS.index(user) + p + 1

        block = ctx.enter_context(nc.Block())

        @block.sync
        def _(sp):
            sp.sem_inc(raw_free, RAW)
            with sp.Fori(0, 7) as s:
                with sp.Fori(0, PANELS) as p:
                    for q in range(PIECES):
                        n = sp.snap((s * PANELS + p) * PIECES + (q + 1))
                        sp.wait_ge(raw_free, n)
                        sp.dma_start(raw[:, q % RAW, :, :], at[bass.ds(p, 1), q].rearrange("o p j i -> (o p) j i"))\
                          .then_inc(loaded[q % RAW], 16)

        @block.gpsimd
        def _(pool):
            pool.memset(ident[:, :], 0.0).then_inc(consts_up, 1)
            pool.memset(ones[:, :], 1.0).then_inc(consts_up, 1)
            pool.memset(neg_half[:, :], -0.5).then_inc(consts_up, 1)
            pool.wait_ge(consts_up, 3)
            pool.affine_select(out=ident[:, :], in_=ident[:, :], compare_op=ALU.not_equal, fill=1.0,
                               base=0, pattern=[[-1, P]], channel_multiplier=1).then_inc(consts_up, 1)
            pool.tensor_copy(ones_r[:, :], ones[:, :]).then_inc(consts_up, 1)
            pool.sem_inc(flag("staging_free"), 2)
            pool.sem_inc(g_used, KT)
            pool.wait_ge(consts_in, 16 * 10)

            def low_part(s, p, q):
                slot = q % RAW
                pool.wait_ge(hi_ready, piece(s, p, q) + 1)
                if s == HYPER:
                    pool.wait_ge(flag("g_sum_steps"), JT * PIECES * p + JT * (q + 1))
                pool.tensor_tensor(low[:, slot], raw[:, slot], high[:, q % HI].bitcast(F32), ALU.subtract)\
                    .then_inc(lo_pool, 1)

            def finish(s, p, q):
                if s == NORMED and q == 1:
                    pool.wait_ge(xr_in, 16 * xr_count(NORMED, p))
                    pool.wait_ge(flag("normed_acc"), 1 + p)
                    pool.tensor_tensor(rows(t1[:, :]), rows(xr[:, :]), bc(part(s_col, p, KT)), ALU.mult)\
                        .then_inc(flag("normed_sx"), 1)

            def panel(s, p, done, dp):
                for q in range(PIECES):
                    if q in POOL_Q[s]:
                        low_part(s, p, q)
                    finish(done, dp, q)

            panel(SMOOTH, 0, SUMS, 3)
            with pool.Fori(1, PANELS) as p:
                panel(SMOOTH, p, SMOOTH, p - 1)

            pool.wait_ge(flag("z_low"), PANELS)
            with pool.Fori(0, PANELS) as p:
                for k in range(KT):
                    pool.wait_ge(flag("staging_free"), KT * p + k + 1)
                    for src, dst in ((zh, z_tile_h), (zl, z_tile_l)):
                        pool.tensor_copy(dst[k % 2][:, :], src[:, bass.ds(p * PW + k * P, P)].bitcast(F32))\
                            .then_inc(flag("staged"), 1)

            pool.wait_ge(rows_stored, 16 + 16 * PANELS)
            with pool.Fori(0, PANELS) as p:
                for k in range(KT):
                    pool.wait_ge(g_used, KT * p + k + 1)
                    pool.tensor_copy(ids[:, k, :], near_i[:, bass.ds(p * KT + k, 1), :].rearrange("p o k -> p (o k)"))\
                        .then_inc(flag("ids_up"), 1)
                    wait_apart(pool, flag("ids_up"), KT * p + k + 1)
                    for n in range(TOP):
                        pool.indirect_dma_start(
                            out=gathered[:, k, n, :], out_offset=None, in_=scaled_rows[:, :],
                            in_offset=bass.IndirectOffsetOnAxis(ap=ids[:, k, n:n + 1], axis=0),
                        ).then_inc(gathers[k], 16)
                pool.wait_ge(xr_in, 16 * xr_count(KNN, p))
                pool.tensor_tensor(rows(xr[:, :]), rows(xr[:, :]),
                                   b02_bc[:, :].unsqueeze(1).to_broadcast([P, KT, D]), ALU.add)\
                    .then_inc(flag("knn_xb"), 1)

            for s in range(GCN1, NORMED + 1):
                panel(s, 0, s - 1, 3)
                with pool.Fori(1, PANELS) as p:
                    panel(s, p, s, p - 1)
            for q in range(PIECES):
                finish(NORMED, 3, q)

        @block.scalar
        def _(act):
            for dst, src in ((w["w01"], w01), (w["w02"], w02), (w["w11"], w11), (w["w12"], w12), (w["w2"], w2),
                             (w["w3"], w3)):
                act.dma_start(dst[:, :], src).then_inc(consts_in, 16)
            act.dma_start(b02_bc[:, :], b02.partition_broadcast(P)).then_inc(consts_in, 16)
            for i, b in enumerate((b01, b11, b12)):
                act.dma_start(b_cols[:, i:i + 1], b.rearrange("(p o) -> p o", o=1)).then_inc(consts_in, 16)
            act.sem_inc(flag("scores_out"), 4)
            act.wait_ge(consts_in, 16 * 10)
            near_chain = Chain(act, "near_act", 1)

            def high_part(s, p, q):
                act.wait_ge(loaded[q % RAW], slot_use(s, p, q))
                act.wait_ge(raw_free, consumed(s, p, q) - HI)
                act.activation(high[:, q % HI], raw[:, q % RAW], ACT.Copy).then_inc(hi_ready, 1)

            def load_x(user, p):
                act.wait_ge(xr_used, xr_count(user, p))
                if user in (GCN2, HYPER, NORMED):
                    act.wait_ge(x_stored[{GCN2: KNN, HYPER: GCN2, NORMED: HYPER}[user]], 16 + 16 * PANELS)
                act.dma_start(xr[:, :], x_dram[user][bass.ds(p, 1)].rearrange("o p n -> (o p) n")).then_inc(xr_in, 16)

            def store_x(s, p):
                act.wait_ge(flag(f"y_up{s}"), p + 1)
                dst = out if s == NORMED else x_dram[{KNN: GCN2, GCN2: HYPER, HYPER: NORMED}[s]]
                act.dma_start(dst[bass.ds(p, 1)].rearrange("o p n -> (o p) n"), t2[:, :]).then_inc(x_stored[s], 16)

            def read_acc(p, func=ACT.Copy, **kw):
                act.activation(t0[:, :], acc(p), func, **kw).then_inc(acc_free, 1)

            def finish(s, p, q):
                if q == 0 and s in XR_USERS:
                    load_x(s, p)

                if s == SUMS:
                    if q == 1:
                        act.wait_ge(flag("sums_shifted"), p + 1)
                        act.activation(c[:, 0:2, :], c[:, 0:2, :], ACT.Sqrt).then_inc(flag("sums_roots"), 1)
                    if q == 3:
                        act.wait_ge(flag("sums_dx"), p + 1)
                        act.activation(tiles(xh[0], p), rows(t2[:, :]), ACT.Copy).then_inc(flag("sums_xh"), 1)
                    if q == 4:
                        act.wait_ge(flag("sums_d_bc"), p + 1)
                        act.activation(part(d_bc, p, PW), ps[:, E0:E0 + PW], ACT.Copy).then_inc(flag("d_bc_up"), 1)

                if s == SMOOTH:
                    if q == 5:
                        act.wait_ge(flag("smooth_w"), p + 1)
                        act.activation(t1[:, :], e0, ACT.Identity, bias=b_cols[:, 0:1]).then_inc(flag("smooth_b"), 1)
                    if q == 7:
                        act.wait_ge(flag("smooth_z"), p + 1)
                        act.activation(part(zh, p, PW), t1[:, :], ACT.Copy).then_inc(flag("z_high"), 1)
                        act.activation(t2[:, :], t1[:, :], ACT.Square).then_inc(flag("z_square"), 1)
                    if q == 10:
                        act.wait_ge(flag("z_norms"), p + 1)
                        act.activation(part(h_rows, p, PW), e1, ACT.Copy).then_inc(flag("h_high"), 1)
                        act.activation(part(sq_col, p, KT), ps[:, E0:E0 + KT], ACT.Copy).then_inc(flag("sq_col_up"), 1)

                if s == NEAR:
                    if q == 1:
                        near_chain.begin(p)
                        act.wait_ge(flag("near_d2"), p + 1)
                        near_chain.link(act.activation(dist[:, :, :], dist[:, :, :], ACT.Sqrt))
                        act.activation(tiles(near_s, p), dist[:, :, :], ACT.Exp, scale=-0.5)\
                            .then_inc(flag("near_s_up"), 1)
                        near_chain.end()
                    if q == 4:
                        act.wait_ge(flag("near_sums"), p + 1)
                        act.activation(c[:, 0, :], c[:, 0, :], ACT.Sqrt).then_inc(flag("near_roots"), 1)
                    if q == 7:
                        act.wait_ge(flag("near_dx"), p + 1)
                        act.activation(tiles(xh[0], p), rows(t0[:, :]), ACT.Copy).then_inc(flag("near_xh"), 1)
                        act.dma_start(scaled_rows[bass.ds(p * PW, PW), :].rearrange("(t p) d -> p t d", p=P),
                                      rows(t0[:, :])).then_inc(rows_stored, 16)

                if s == KNN:
                    if q == 9:
                        act.wait_ge(flag("knn_acc"), p + 1)
                        read_acc(p)
                    if q == 12:
                        root(s, p)
                    if q == 13:
                        rounded_x(s, p)
                        store_x(s, p)

                if s == GCN1:
                    if q == 1:
                        act.wait_ge(raw_free, consumed(s, p, PIECES - 1))
                        read_acc(p)
                    if q == 5:
                        act.wait_ge(flag("gcn1_w"), p + 1)
                        act.activation(t1[:, :], e0, ACT.Relu, bias=b_cols[:, 1:2]).then_inc(flag("gcn1_h"), 1)
                    if q == 9:
                        act.wait_ge(flag("gcn1_rows"), p + 1)
                        act.activation(tiles(xh[BUF[GCN2]], p), rows(e1), ACT.Copy).then_inc(flag("gcn1_xh"), 1)

                if s == GCN2:
                    if q == 1:
                        act.wait_ge(raw_free, consumed(s, p, PIECES - 1))
                        read_acc(p, ACT.Relu, bias=b_cols[:, 2:3])
                    if q == 5:
                        root(s, p)
                    if q == 6:
                        act.wait_ge(flag(f"y_up{s}"), p + 1)
                        store_x(s, p)
                        act.activation(t1[:, :], t2[:, :], ACT.Square).then_inc(flag("gcn2_x_sq"), 1)
                    if q == 8:
                        act.wait_ge(flag("gcn2_xt"), p + 1)
                        act.activation(t0[:, :], e1, ACT.Copy).then_inc(flag("gcn2_xt_read"), 1)
                    if q == 10:
                        act.wait_ge(flag("gcn2_mx"), p + 1)
                        act.wait_ge(flag("gcn2_x_norm"), p + 1)
                        act.activation(t1[:, :], e0, ACT.Square).then_inc(flag("gcn2_mx_sq"), 1)
                        act.wait_ge(flag("gcn2_mx_norm"), p + 1)
                        act.activation(c[:, 2:4, :], c[:, 0:2, :], ACT.Sqrt).then_inc(flag("gcn2_roots"), 1)
                    if q == 11:
                        act.wait_ge(flag("gcn2_ratio"), p + 1)
                        act.activation(c[:, 5, :], c[:, 5, :], ACT.Ln).then_inc(flag("gcn2_ln"), 1)
                        act.wait_ge(flag("gcn2_arg"), p + 1)
                        act.activation(c[:, 5, :], c[:, 5, :], ACT.Tanh).then_inc(flag("gcn2_tanh"), 1)
                        rounded_x(s, p)

                if s == HYPER:
                    if q == 1:
                        act.wait_ge(raw_free, consumed(s, p, PIECES - 1))
                        read_acc(p)
                    if q == 3:
                        act.wait_ge(flag("hyper_rows"), p + 1)
                        act.activation(t1[:, :], e0, ACT.Square).then_inc(flag("hyper_sq"), 1)
                    if q == 4:
                        act.wait_ge(flag("hyper_norm"), p + 1)
                        act.activation(c[:, 0, :], c[:, 0, :], ACT.Sqrt).then_inc(flag("hyper_root"), 1)
                    if q in (5, 7, 9):
                        n = (q - 5) // 2
                        act.wait_ge(flag("hyper_ratio"), 3 * p + n + 1)
                        act.activation(c[:, 5, :], c[:, 5, :], ACT.Ln).then_inc(flag("hyper_ln"), 1)
                    if q in (6, 8):
                        n = (q - 6) // 2
                        act.wait_ge(flag("hyper_arg"), 2 * p + n + 1)
                        act.activation(c[:, 5, :], c[:, 5, :], ACT.Tanh).then_inc(flag("hyper_tanh"), 1)
                    if q == 10:
                        act.wait_ge(flag("hyper_u"), p + 1)
                        act.activation(t0[:, :], t1[:, :], ACT.Square).then_inc(flag("hyper_u_sq"), 1)
                        act.wait_ge(flag("hyper_u_norm"), p + 1)
                        act.activation(c[:, 0, :], c[:, 0, :], ACT.Sqrt).then_inc(flag("hyper_u_root"), 1)
                    if q == 11:
                        act.wait_ge(flag("hyper_un"), p + 1)
                        act.activation(c[:, 1, :], c[:, 0, :], ACT.Tanh).then_inc(flag("hyper_u_tanh"), 1)
                    if q == 12:
                        root(s, p)
                    if q == 13:
                        store_x(s, p)
                        rounded_x(s, p)

                if s == NORMED:
                    if q == 4:
                        act.wait_ge(flag("normed_acc"), 1 + p + 1)
                        read_acc(p)
                    if q == 8:
                        root(s, p)
                    if q == 9:
                        store_x(s, p)

            def root(s, p):
                act.wait_ge(flag(f"var_up{s}"), p + 1)
                act.activation(c[:, 14, :], c[:, 14, :], ACT.Sqrt).then_inc(flag(f"root_up{s}"), 1)

            def rounded_x(s, p):
                src = {KNN: t2, GCN2: t1, HYPER: t0}[s]
                act.wait_ge(flag(f"new_x{s}"), p + 1)
                act.activation(tiles(xh[BUF[s + 1]], p), rows(src[:, :]), ACT.Copy).then_inc(flag(f"new_xh{s}"), 1)

            def panel(s, p, done, dp):
                for q in range(PIECES):
                    high_part(s, p, q)
                    finish(done, dp, q)

            with act.Fori(0, PANELS - 1) as p:
                for q in range(PIECES):
                    finish(SUMS, p, q)
            panel(SMOOTH, 0, SUMS, 3)
            with act.Fori(1, PANELS) as p:
                panel(SMOOTH, p, SMOOTH, p - 1)
            for q in range(PIECES):
                finish(SMOOTH, 3, q)

            def scores_out(p, q):
                k = q // 2
                if q % 2 == 0:
                    act.wait_ge(flag("searched"), KT * p + k + 1)
                for r in range(2):
                    pair = q % 2 * 2 + r
                    act.wait_ge(flag("scores_up"), 4 * (KT * p + k) + pair + 1)
                    act.activation(scores[k % 2][:, pair * PW:(pair + 1) * PW], ps[:, pair * PW:(pair + 1) * PW],
                                   ACT.Copy).then_inc(flag("scores_out"), 1)

            for q in range(PIECES):
                scores_out(0, q)
            with act.Fori(1, PANELS) as p:
                for q in range(PIECES):
                    scores_out(p, q)
                    finish(NEAR, p - 1, q)

            act.wait_ge(flag("searched"), 2 + N // P)
            panel(KNN, 0, NEAR, 3)
            with act.Fori(1, PANELS) as p:
                panel(KNN, p, KNN, p - 1)
            for s in range(GCN1, NORMED + 1):
                panel(s, 0, s - 1, 3)
                with act.Fori(1, PANELS) as p:
                    panel(s, p, s, p - 1)
            for q in range(PIECES):
                finish(NORMED, 3, q)
            act.wait_ge(x_stored[NORMED], 16 + 16 * PANELS)

        @block.vector
        def _(dve):
            TT, TS, STT = dve.tensor_tensor, dve.tensor_scalar, dve.scalar_tensor_tensor
            sums = Chain(dve, "sums_dve", PIECES)
            near = Chain(dve, "near_dve", 3)
            picks = Chain(dve, "picks_dve", TOP * KT)
            ln = {s: Chain(dve, f"norm_dve{s}", n) for s, n in
                  ((KNN, 2 + 2 * KT + 1), (GCN2, 2 * KT + 1), (HYPER, 2 * KT + 1), (NORMED, 2 + 2 * KT + 1))}
            mob = Chain(dve, "mobius_dve", 16)
            hyp = Chain(dve, "hyper_dve", 40)
            dve.sem_inc(flag("searched"), 2)
            dve.sem_inc(acc_free, 2)
            for which in (xr_used, *(flag(n) for n in ("normed_acc", "g_whole_up", "hyper_den", "sums_read"))):
                dve.sem_inc(which, 1)
            for which in (rows_stored, *x_stored.values()):
                dve.sem_inc(which, 16)
            dve.wait_ge(consts_in, 16 * 10)
            dve.wait_ge(consts_up, 5)

            def add_piece(p, q):
                dve.wait_ge(loaded[q % RAW], slot_use(SUMS, p, q))
                if q == 0:
                    dve.wait_ge(flag("sums_read"), 1 + p)
                    sums.begin(p)
                    ins = dve.tensor_copy(a_sum[:, :, :], raw[:, 0])
                else:
                    ins = TT(a_sum[:, :, :], a_sum[:, :, :], raw[:, q % RAW], ALU.add)
                ins.then_inc(raw_free, 1)
                dve.wait_ge(raw_free, RAW + PIECES * p + q + 1)

            def low_part(s, p, q):
                slot = q % RAW
                dve.wait_ge(hi_ready, piece(s, p, q) + 1)
                if s == HYPER:
                    dve.wait_ge(flag("g_sum_steps"), JT * PIECES * p + JT * (q + 1))
                TT(low[:, slot], raw[:, slot], high[:, q % HI].bitcast(F32), ALU.subtract).then_inc(lo_dve, 1)

            def weigh_piece(p, q):
                dve.wait_ge(hi_ready, piece(HYPER, p, q) + 1)
                for j in range(JT):
                    n = JT * q + j
                    if n == 0:
                        dve.wait_ge(flag("g_whole_up"), 1 + p)
                        ins = TS(g_sum[:, :], raw[:, 0, 0], g_col[:, 0:1], None, ALU.mult)
                    else:
                        dve.wait_ge(flag("g_sum_steps"), JT * PIECES * p + n)
                        ins = STT(g_sum[:, :], raw[:, q % RAW, j], g_col[:, n:n + 1], g_sum[:, :], ALU.mult, ALU.add)
                    ins.then_inc(flag("g_sum_steps"), 1)
                if q == PIECES - 1:
                    dve.wait_ge(flag("g_sum_steps"), JT * PIECES * (p + 1))
                    dve.wait_ge(flag("hyper_den"), 1 + p)
                    dve.tensor_copy(g_whole[:, :], g_sum[:, :]).then_inc(flag("g_whole_up"), 1)

            def variances(s, p, src):
                ch = ln[s]
                ch.link(*[dve.bn_stats(stats[:, k, :], rows(src[:, :])[:, k, :]) for k in range(KT)], apart=True)
                ch.link(*[dve.bn_aggr(mv[:, k, :], stats[:, k, :]) for k in range(KT)])
                TS(c[:, 14, :], mv[:, :, 1], LN_EPS, None, ALU.add).then_inc(flag(f"var_up{s}"), 1)

            def normalise(s, p, src):
                ch = ln[s]
                dve.wait_ge(flag(f"root_up{s}"), p + 1)
                ch.link(dve.reciprocal(c[:, 15, :], c[:, 14, :]))
                ch.end()
                dve.wait_ge(x_stored[s], 16 + 16 * p)
                if s == KNN:
                    dve.wait_ge(flag("knn_acc"), p + 1)
                for k in range(KT):
                    last = TS(rows(t2[:, :])[:, k, :], rows(src[:, :])[:, k, :], mv[:, k, 0:1], c[:, 15, k:k + 1],
                              ALU.subtract, ALU.mult)
                    if k < KT - 1:
                        last.then_inc(flag(f"y_part{s}"), 1)
                dve.wait_ge(flag(f"y_part{s}"), (KT - 1) * (p + 1))
                last.then_inc(flag(f"y_up{s}"), 1)

            def rest_of_x(s, p, src):
                dve.wait_ge(flag(f"new_xh{s}"), p + 1)
                TT(tiles(xl[BUF[s + 1]], p), rows(src[:, :]), tiles(xh[BUF[s + 1]], p).bitcast(F32), ALU.subtract)\
                    .then_inc(x_ready[s + 1], 1)
                dve.wait_ge(x_ready[s + 1], p + 1)

            def ratio(chain, src, lo, hi):
                chain.link(TS(c[:, lo, :], c[:, src, :], CLIP, None, ALU.min))
                chain.link(TS(c[:, hi, :], c[:, lo, :], 1.0, None, ALU.add),
                           TS(c[:, lo + 1, :], c[:, lo, :], -1.0, 1.0, ALU.mult, ALU.add))
                chain.link(dve.reciprocal(c[:, lo + 1, :], c[:, lo + 1, :]))
                return TT(c[:, hi, :], c[:, hi, :], c[:, lo + 1, :], ALU.mult)

            def finish(s, p, q):
                if s == SUMS:
                    if q == 0:
                        dve.wait_ge(flag("sums_read"), 1 + p + 1)
                        dve.tensor_copy(part(a_rows, p, KT), ps[:, E1:E1 + KT]).then_inc(flag("a_rows_up"), 1)
                        dve.tensor_copy(c[:, 0, :], ps[:, E1:E1 + KT]).then_inc(flag("a_rows_up"), 1)
                        TS(c[:, 1, :], ps[:, E1:E1 + KT], L3_EPS, None, ALU.add).then_inc(flag("sums_shifted"), 1)
                    if q == 2:
                        dve.wait_ge(flag("sums_roots"), p + 1)
                        dve.reciprocal(part(s_col, p, KT), c[:, 1, :]).then_inc(flag("s_col_up"), 1)
                        dve.reciprocal(part(d_col, p, KT), c[:, 0, :]).then_inc(flag("d_col_up"), 1)
                        dve.wait_ge(flag("d_col_up"), p + 1)
                        dve.wait_ge(xr_in, 16 * xr_count(SUMS, p))
                        TT(rows(t2[:, :]), rows(xr[:, :]), bc(part(d_col, p, KT)), ALU.mult).then_inc(flag("sums_dx"), 1)
                    if q == 3:
                        dve.wait_ge(flag("sums_xh"), p + 1)
                        TT(tiles(xl[0], p), rows(t2[:, :]), tiles(xh[0], p).bitcast(F32), ALU.subtract)\
                            .then_inc(x_ready[SMOOTH], 1)
                        dve.wait_ge(x_ready[SMOOTH], p + 1)
                        TT(rows(xr[:, :]), ident[:, :].unsqueeze(1).to_broadcast([P, KT, P]),
                           bc(part(d_col, p, KT), P), ALU.mult).then_inc(flag("sums_diag"), 1)

                if s == SMOOTH:
                    if q == 1:
                        dve.wait_ge(raw_free, consumed(s, p, PIECES - 1))
                        dve.wait_ge(flag("d_bc_up"), PANELS)
                        TT(t0[:, :], acc(p), part(d_bc, p, PW), ALU.mult).then_inc(acc_free, 1)
                    if q == 6:
                        dve.wait_ge(flag("smooth_b"), p + 1)
                        STT(t1[:, :], t1[:, :], 0.1, t1[:, :], ALU.mult, ALU.max).then_inc(flag("smooth_z"), 1)
                    if q == 8:
                        dve.wait_ge(flag("z_high"), p + 1)
                        TT(part(zl, p, PW), t1[:, :], part(zh, p, PW).bitcast(F32), ALU.subtract)\
                            .then_inc(flag("z_low"), 1)
                    if q == 11:
                        dve.wait_ge(flag("h_high"), p + 1)
                        h = part(h_rows, p, PW)
                        TT(t2[:, :], e1, h.bitcast(F32), ALU.subtract).then_inc(flag("h_low"), 1)
                        dve.wait_ge(flag("h_low"), 2 * p + 1)
                        TS(t2[:, :], t2[:, :], ident[:, 1:2], None, ALU.mult).then_inc(flag("h_low"), 1)
                        dve.wait_ge(flag("h_low"), 2 * p + 2)
                        STT(h, h.bitcast(F32), ident[:, 0:1], t2[:, :], ALU.mult, ALU.add).then_inc(flag("h_up"), 1)

                if s == NEAR:
                    if q == 0:
                        near.begin(p)
                        dve.wait_ge(flag("sq_col_up"), PANELS)
                        near.link(STT(dist[:, :, :], top_v[:, :, 0:TOP], -2.0, bc(part(sq_col, p, KT), TOP),
                                      ALU.mult, ALU.add))
                        TS(dist[:, :, :], dist[:, :, :], 0.0, TINY, ALU.max, ALU.add).then_inc(flag("near_d2"), 1)
                        near.link(dve.tensor_copy(tiles(near_i, p), top_i[:, :, 0:TOP]))
                    if q == 3:
                        dve.wait_ge(flag("near_s_up"), p + 1)
                        near.link(dve.tensor_reduce(out=c[:, 1, :], in_=tiles(near_s, p), op=ALU.add, axis=AX.X))
                        near.end()
                        TT(c[:, 0, :], c[:, 1, :], part(a_rows, p, KT), ALU.add).then_inc(flag("near_sums"), 1)
                    if q == 6:
                        dve.wait_ge(flag("near_roots"), p + 1)
                        dve.reciprocal(part(d2_col, p, KT), c[:, 0, :]).then_inc(flag("d2_col_up"), 1)
                        dve.wait_ge(flag("d2_col_up"), p + 1)
                        dve.wait_ge(xr_in, 16 * xr_count(NEAR, p))
                        dve.wait_ge(rows_stored, 16 + 16 * p)
                        TT(rows(t0[:, :]), rows(xr[:, :]), bc(part(d2_col, p, KT)), ALU.mult)\
                            .then_inc(flag("near_dx"), 1)
                    if q == 8:
                        dve.wait_ge(flag("near_xh"), p + 1)
                        TT(tiles(xl[0], p), rows(t0[:, :]), tiles(xh[0], p).bitcast(F32), ALU.subtract)\
                            .then_inc(x_ready[KNN], 1)
                        dve.wait_ge(x_ready[KNN], p + 1)
                        dve.sem_inc(xr_used, 1)

                if s == KNN:
                    if q == 0:
                        picks.begin(p)
                    if q < KT:
                        dve.wait_ge(gathers[q], 16 * TOP * (p + 1))
                        y = rows(t2[:, :])[:, q, :]
                        if q == 0:
                            dve.wait_ge(x_stored[KNN], 16 + 16 * p)
                        for n in range(TOP):
                            weight = near_s[:, bass.ds(p * KT + q, 1), n:n + 1].rearrange("p o k -> p (o k)")
                            if n == 0:
                                picks.link(TS(y, gathered[:, q, 0, :], weight, None, ALU.mult))
                            else:
                                picks.link(STT(y, gathered[:, q, n, :], weight, y, ALU.mult, ALU.add))
                        dve.sem_inc(g_used, 1)
                        if q == KT - 1:
                            picks.end()
                            dve.sem_inc(flag("picked"), 1)
                    if q == 11:
                        dve.wait_ge(flag("knn_rows"), p + 1)
                        dve.wait_ge(flag("knn_xb"), p + 1)
                        ch = ln[s]
                        ch.begin(p)
                        ch.link(TT(rows(t1[:, :]), rows(e0), bc(part(d2_col, p, KT)), ALU.mult))
                        ch.link(TT(t1[:, :], t1[:, :], xr[:, :], ALU.add))
                        dve.sem_inc(xr_used, 1)
                        variances(s, p, t1)
                    if q == 12:
                        normalise(s, p, t1)
                        dve.wait_ge(flag(f"y_up{s}"), p + 1)
                        dve.sem_inc(flag(f"new_x{s}"), 1)
                    if q == 13:
                        rest_of_x(s, p, t2)

                if s == GCN1:
                    if q == 10:
                        dve.wait_ge(flag("gcn1_xh"), p + 1)
                        TT(tiles(xl[BUF[GCN2]], p), rows(e1), tiles(xh[BUF[GCN2]], p).bitcast(F32), ALU.subtract)\
                            .then_inc(x_ready[GCN2], 1)

                if s == GCN2:
                    if q == 4:
                        dve.wait_ge(flag("gcn2_rows"), p + 1)
                        dve.wait_ge(xr_in, 16 * xr_count(s, p))
                        ln[s].begin(p)
                        TT(t1[:, :], e0, xr[:, :], ALU.add).then_inc(xr_used, 1)
                        dve.wait_ge(xr_used, 1 + xr_count(s, p))
                        variances(s, p, t1)
                    if q == 5:
                        normalise(s, p, t1)
                    if q == 8:
                        dve.wait_ge(flag("gcn2_x_sq"), p + 1)
                        dve.tensor_reduce(out=c[:, 0, :], in_=rows(t1[:, :]), op=ALU.add, axis=AX.X)\
                           .then_inc(flag("gcn2_x_norm"), 1)
                    if q == 10:
                        mob.begin(p)
                        dve.wait_ge(flag("gcn2_mx_sq"), p + 1)
                        dve.tensor_reduce(out=c[:, 1, :], in_=rows(t1[:, :]), op=ALU.add, axis=AX.X)\
                           .then_inc(flag("gcn2_mx_norm"), 1)
                        dve.wait_ge(flag("gcn2_roots"), p + 1)
                        mob.link(TS(c[:, 2:4, :], c[:, 2:4, :], MIN_NORM, None, ALU.max))
                        ratio(mob, 2, 8, 5).then_inc(flag("gcn2_ratio"), 1)
                        mob.link(dve.reciprocal(c[:, 6:8, :], c[:, 2:4, :]))
                        mob.link(TT(c[:, 6, :], c[:, 6, :], c[:, 3, :], ALU.mult))
                    if q == 11:
                        dve.wait_ge(flag("gcn2_ln"), p + 1)
                        STT(c[:, 5, :], c[:, 5, :], 0.5, c[:, 6, :], ALU.mult, ALU.mult).then_inc(flag("gcn2_arg"), 1)
                        dve.wait_ge(flag("gcn2_tanh"), p + 1)
                        mob.link(TT(c[:, 5, :], c[:, 5, :], c[:, 7, :], ALU.mult))
                        mob.link(TT(c[:, 10, :], c[:, 1, :], c[:, 5, :], ALU.mult))
                        mob.link(TT(c[:, 10, :], c[:, 10, :], c[:, 5, :], ALU.mult))
                        mob.link(TS(c[:, 10, :], c[:, 10, :], -1.0, 1.0, ALU.mult, ALU.add))
                        mob.link(TS(c[:, 10, :], c[:, 10, :], 1e-5, None, ALU.max))
                        mob.link(dve.reciprocal(c[:, 10, :], c[:, 10, :]))
                        mob.link(TS(c[:, 10, :], c[:, 10, :], 2.0, None, ALU.mult))
                        mob.link(TS(part(g_col, p, KT), c[:, 10, :], -1.0, None, ALU.add))
                        mob.link(TT(c[:, 10, :], c[:, 10, :], c[:, 5, :], ALU.mult))
                        mob.end()
                        TT(rows(t1[:, :]), rows(e0), bc(c[:, 10, :]), ALU.mult).then_inc(flag(f"new_x{s}"), 1)
                        rest_of_x(s, p, t1)

                if s == HYPER:
                    if q == 4:
                        hyp.begin(p)
                        den = ps[:, E1:E1 + KT]
                        dve.wait_ge(flag("hyper_den"), 1 + p + 1)
                        hyp.link(TS(c[:, 2, :], den, TINY, None, ALU.max), TS(c[:, 3, :], den, -TINY, None, ALU.min),
                                 TS(c[:, 4, :], den, 0.0, None, ALU.is_ge))
                        hyp.link(TT(c[:, 2, :], c[:, 2, :], c[:, 3, :], ALU.subtract))
                        hyp.link(TT(c[:, 2, :], c[:, 2, :], c[:, 4, :], ALU.mult))
                        hyp.link(TT(c[:, 2, :], c[:, 2, :], c[:, 3, :], ALU.add))
                        hyp.link(dve.reciprocal(c[:, 2, :], c[:, 2, :]))
                        dve.wait_ge(flag("hyper_sq"), p + 1)
                        dve.tensor_reduce(out=c[:, 0, :], in_=rows(t1[:, :]), op=ALU.add, axis=AX.X)\
                           .then_inc(flag("hyper_norm"), 1)
                        dve.wait_ge(flag("hyper_root"), p + 1)
                        hyp.link(TT(c[:, 1, :], c[:, 0, :], c[:, 2, :], ALU.mult))
                        hyp.link(STT(c[:, 1, :], c[:, 1, :], -1.0, c[:, 1, :], ALU.mult, ALU.max))
                        bounded(1)
                    if q == 6:
                        dve.wait_ge(flag("hyper_ln"), 3 * p + 1)
                        TS(c[:, 5, :], c[:, 5, :], 0.25, None, ALU.mult).then_inc(flag("hyper_arg"), 1)
                        dve.wait_ge(flag("hyper_tanh"), 2 * p + 1)
                        scaled()
                        bounded(1)
                    if q == 8:
                        dve.wait_ge(flag("hyper_ln"), 3 * p + 2)
                        STT(c[:, 5, :], c[:, 5, :], 0.5, part(a_rows, p, KT), ALU.mult, ALU.mult)\
                            .then_inc(flag("hyper_arg"), 1)
                        dve.wait_ge(flag("hyper_tanh"), 2 * p + 2)
                        scaled()
                        hyp.link(STT(c[:, 1, :], c[:, 1, :], -1.0, c[:, 1, :], ALU.mult, ALU.max))
                        bounded(1)
                    if q == 10:
                        dve.wait_ge(flag("hyper_ln"), 3 * p + 3)
                        hyp.link(STT(c[:, 5, :], c[:, 5, :], 0.5, c[:, 7, :], ALU.mult, ALU.mult))
                        hyp.link(TT(c[:, 2, :], c[:, 2, :], c[:, 5, :], ALU.mult))
                        hyp.link(TT(rows(t1[:, :]), rows(e0), bc(c[:, 2, :]), ALU.mult))
                        TS(t1[:, :], t1[:, :], 0.0, None, ALU.max).then_inc(flag("hyper_u"), 1)
                        dve.wait_ge(flag("hyper_u_sq"), p + 1)
                        dve.tensor_reduce(out=c[:, 0, :], in_=rows(t0[:, :]), op=ALU.add, axis=AX.X)\
                           .then_inc(flag("hyper_u_norm"), 1)
                        dve.wait_ge(flag("hyper_u_root"), p + 1)
                        TS(c[:, 0, :], c[:, 0, :], MIN_NORM, None, ALU.max).then_inc(flag("hyper_un"), 1)
                        dve.wait_ge(flag("hyper_un"), p + 1)
                        hyp.link(dve.reciprocal(c[:, 3, :], c[:, 0, :]))
                        dve.wait_ge(flag("hyper_u_tanh"), p + 1)
                        hyp.link(TT(c[:, 3, :], c[:, 3, :], c[:, 1, :], ALU.mult))
                        hyp.link(TT(rows(t1[:, :]), rows(t1[:, :]), bc(c[:, 3, :]), ALU.mult))
                        hyp.end()
                        dve.wait_ge(xr_in, 16 * xr_count(s, p))
                        TT(t1[:, :], t1[:, :], xr[:, :], ALU.add).then_inc(xr_used, 1)
                        dve.wait_ge(xr_used, 1 + xr_count(s, p))
                        ln[s].begin(p)
                        variances(s, p, t1)
                    if q == 12:
                        normalise(s, p, t1)
                        dve.wait_ge(flag(f"y_up{s}"), p + 1)
                        TT(rows(t0[:, :]), rows(t2[:, :]), bc(part(s_col, p, KT)), ALU.mult)\
                            .then_inc(flag(f"new_x{s}"), 1)
                    if q == 14:
                        rest_of_x(s, p, t0)

                if s == NORMED:
                    if q == 7:
                        dve.wait_ge(flag("normed_rows"), p + 1)
                        ch = ln[s]
                        ch.begin(p)
                        ch.link(TT(rows(t1[:, :]), rows(e0), bc(part(s_col, p, KT)), ALU.mult))
                        ch.link(TT(t1[:, :], t1[:, :], xr[:, :], ALU.add))
                        dve.sem_inc(xr_used, 1)
                        variances(s, p, t1)
                    if q == 8:
                        normalise(s, p, t1)

            def bounded(src):
                hyp.link(TS(c[:, 6, :], c[:, src, :], MIN_NORM, None, ALU.max))
                hyp.link(dve.reciprocal(c[:, 7, :], c[:, 6, :]))
                ratio(hyp, 6, 8, 5).then_inc(flag("hyper_ratio"), 1)

            def scaled():
                hyp.link(TT(c[:, 5, :], c[:, 5, :], c[:, 7, :], ALU.mult))
                hyp.link(TT(c[:, 2, :], c[:, 2, :], c[:, 5, :], ALU.mult), TT(c[:, 1, :], c[:, 1, :], c[:, 5, :], ALU.mult))

            def panel(s, p, done, dp):
                for q in range(PIECES):
                    if s == HYPER:
                        weigh_piece(p, q)
                    if q not in POOL_Q[s]:
                        low_part(s, p, q)
                    finish(done, dp, q)

            for q in range(PIECES):
                add_piece(0, q)
            with dve.Fori(1, PANELS) as p:
                for q in range(PIECES):
                    add_piece(p, q)
                    finish(SUMS, p - 1, q - 4)
            panel(SMOOTH, 0, SUMS, 3)
            with dve.Fori(1, PANELS) as p:
                panel(SMOOTH, p, SMOOTH, p - 1)
            for q in range(PIECES):
                finish(SMOOTH, 3, q)

            def search(p, k):
                wait_apart(dve, flag("scores_out"), 4 + 4 * (KT * p + k + 1))
                dve.max(out=top_v[:, k, :], in_=scores[k % 2][:, :]).then_inc(flag("maxima"), 1)
                wait_apart(dve, flag("maxima"), KT * p + k + 1)
                dve.max_index(out=top_i[:, k, :], in_max=top_v[:, k, :], in_values=scores[k % 2][:, :])\
                   .then_inc(flag("searched"), 1)

            for k in range(KT):
                search(0, k)
            with dve.Fori(1, PANELS) as p:
                dve.wait_ge(flag("searched"), 2 + KT * p)
                finish(NEAR, p - 1, 0)
                for k in range(KT):
                    search(p, k)
                    for q in (2 * k + 1, 2 * k + 2):
                        finish(NEAR, p - 1, q)
            dve.wait_ge(flag("searched"), 2 + N // P)
            panel(KNN, 0, NEAR, 3)
            with dve.Fori(1, PANELS) as p:
                panel(KNN, p, KNN, p - 1)
            for s in range(GCN1, NORMED + 1):
                panel(s, 0, s - 1, 3)
                with dve.Fori(1, PANELS) as p:
                    panel(s, p, s, p - 1)
            for q in range(PIECES):
                finish(NORMED, 3, q)

        @block.tensor
        def _(pe):
            mm = pe.matmul
            pe.wait_ge(consts_in, 16 * 10)
            pe.wait_ge(consts_up, 5)

            def chunk(t, i):
                return t[:, i * BANK:(i + 1) * BANK]

            def by_weights(name, src, weights):
                for i in range(CH):
                    last = mm(chunk(e0, i), weights[:, :], chunk(src, i), start=True, stop=True)
                last.then_inc(flag(name), 1)

            def by_tiles(name, dst, src, right):
                for k in range(KT):
                    last = mm(dst[:, k * D:(k + 1) * D], src[:, k * P:(k + 1) * P], right[:, :], start=True, stop=True)
                last.then_inc(flag(name), 1)

            def turned(name, dst, src):
                for k in range(KT):
                    last = pe.transpose(dst[:, k * D:(k + 1) * D], src[:, k * P:(k + 1) * P], ident[:, :])
                last.then_inc(flag(name), 1)

            def sums_down(name, col, *srcs):
                for k in range(KT):
                    for i, src in enumerate(srcs):
                        last = mm(ps[:, col + k:col + k + 1], src[:, k * P:(k + 1) * P], ones[:, 0:1],
                                  start=i == 0, stop=i == len(srcs) - 1)
                last.then_inc(flag(name), 1)

            def add_turned(name, p, src):
                for k in range(KT):
                    last = mm(acc(p, k * P, P), src[:, k * P:(k + 1) * P], ident[:, :], start=False,
                              stop=k % (BANK // P) == BANK // P - 1)
                last.then_inc(flag(name), 1)

            def product(s, p, q):
                b, slot, stays = BUF[s], q % RAW, s in (KNN, NORMED)
                if q == 0 and not (s == SMOOTH and isinstance(p, int)):
                    pe.wait_ge(acc_free, evictions(s, p) - 2)
                if q % 4 == 0 and isinstance(p, int):
                    pe.wait_ge(x_ready[s], q // 4 + 1)
                pe.wait_ge(hi_ready, piece(s, p, q) + 1)
                for j in range(JT):
                    for x_part in (xh[b], xl[b]):
                        for i in range(CH):
                            mm(acc(p, i * BANK, BANK), x_part[:, JT * q + j, :], chunk(high[:, q % HI, j], i),
                               start=(q, j) == (0, 0) and x_part is xh[b], stop=False)
                by_pool, count = low_count(s, p, q)
                pe.wait_ge(lo_pool if by_pool else lo_dve, count)
                for j in range(JT):
                    for i in range(CH):
                        last = mm(acc(p, i * BANK, BANK), xh[b][:, JT * q + j, :], chunk(low[:, slot, j], i),
                                  start=False, stop=(q, j) == (PIECES - 1, JT - 1) and not stays)
                last.then_inc(raw_free, 1)

            def finish(s, p, q):
                if s == SUMS:
                    if q == 4:
                        pe.wait_ge(flag("sums_diag"), p + 1)
                        for i in range(CH):
                            last = mm(chunk(e0, i), ones[:, :], chunk(xr, i), start=True, stop=True)
                        last.then_inc(flag("sums_d_bc"), 1)
                        pe.wait_ge(flag("sums_d_bc"), p + 1)
                        pe.sem_inc(xr_used, 1)
                if s == SMOOTH:
                    if q == 3:
                        pe.wait_ge(acc_free, evictions(s, p))
                        by_weights("smooth_w", t0, w["w01"])
                    if q == 9:
                        pe.wait_ge(flag("z_square"), p + 1)
                        for i in range(CH):
                            mm(chunk(e1, i), neg_half[:, :], chunk(t2, i), start=True, stop=True)
                        sums_down("z_norms", E0, t2)
                if s == KNN:
                    if q == 8:
                        pe.wait_ge(flag("picked"), p + 1)
                        add_turned("knn_acc", p, t2)
                    if q == 10:
                        pe.wait_ge(acc_free, evictions(s, p))
                        by_tiles("knn_rows", e0, t0, w["w02"])
                if s == GCN1:
                    if q == 3:
                        pe.wait_ge(acc_free, evictions(s, p))
                        by_weights("gcn1_w", t0, w["w11"])
                    if q == 7:
                        pe.wait_ge(flag("gcn1_h"), p + 1)
                        by_tiles("gcn1_rows", e1, t1, w["w12"])
                if s == GCN2:
                    if q == 3:
                        pe.wait_ge(acc_free, evictions(s, p))
                        turned("gcn2_rows", e0, t0)
                    if q == 7:
                        pe.wait_ge(flag(f"y_up{s}"), p + 1)
                        turned("gcn2_xt", e1, t2)
                    if q == 9:
                        pe.wait_ge(flag("gcn2_xt_read"), p + 1)
                        by_tiles("gcn2_mx", e0, t0, w["w2"])
                if s == HYPER:
                    if q == 0:
                        pe.wait_ge(flag("g_whole_up"), 1 + p + 1)
                        sums_down("hyper_den", E1, g_whole)
                    if q == 2:
                        pe.wait_ge(acc_free, evictions(s, p))
                        turned("hyper_rows", e0, t0)
                if s == NORMED:
                    if q == 2:
                        pe.wait_ge(flag("normed_sx"), p + 1)
                        add_turned("normed_acc", p, t1)
                    if q == 6:
                        pe.wait_ge(acc_free, evictions(s, p))
                        by_tiles("normed_rows", e0, t0, w["w3"])

            def panel(s, p, done, dp):
                for q in range(PIECES):
                    finish(done, dp, q)
                    product(s, p, q)

            def read_sums(p):
                pe.wait_ge(raw_free, RAW + PIECES * (p + 1))
                sums_down("sums_read", E1, a_sum[:, 0], a_sum[:, 1])

            read_sums(0)
            with pe.Fori(1, PANELS) as p:
                finish(SUMS, p - 1, 4)
                read_sums(p)
            panel(SMOOTH, 0, SUMS, 3)
            with pe.Fori(1, PANELS) as p:
                panel(SMOOTH, p, SMOOTH, p - 1)
            for q in range(PIECES):
                finish(SMOOTH, 3, q)

            pe.wait_ge(flag("h_up"), PANELS)
            pe.wait_ge(flag("z_low"), PANELS)
            pe.wait_ge(flag("sq_col_up"), PANELS)
            with pe.Fori(0, PANELS) as p:
                for k in range(KT):
                    pe.wait_ge(flag("staged"), 2 * (KT * p + k + 1))
                    for i in range(8):
                        if i % CH == 0:
                            pe.wait_ge(flag("scores_out"), 4 * (KT * p + k) + i // CH + 1)
                        dst = chunk(ps, i)
                        mm(dst, z_tile_h[k % 2][:, :], chunk(zh, i), start=True, stop=False)
                        mm(dst, z_tile_h[k % 2][:, :], chunk(zl, i), start=False, stop=False)
                        last = mm(dst, z_tile_l[k % 2][:, :], chunk(zh, i), start=False, stop=False)
                        if i == 7:
                            last.then_inc(flag("staging_free"), 1)
                        last = mm(dst, ones_r[:, :], chunk(h_rows, i), start=False, stop=True)
                        if i % CH == CH - 1:
                            last.then_inc(flag("scores_up"), 1)

            pe.wait_ge(flag("scores_out"), 4 + 4 * N // P)
            panel(KNN, 0, NEAR, 3)
            with pe.Fori(1, PANELS) as p:
                panel(KNN, p, KNN, p - 1)
            for s in range(GCN1, NORMED + 1):
                panel(s, 0, s - 1, 3)
                with pe.Fori(1, PANELS) as p:
                    panel(s, p, s, p - 1)
            for q in range(PIECES):
                finish(NORMED, 3, q)


def kernel(**inputs):
    import numpy as np
    import concourse.bacc as bacc
    from concourse.bass_utils import run_bass_kernel_spmd as run

    nc = bacc.Bacc("TRN2", target_bir_lowering=False, num_devices=1)
    at = np.ascontiguousarray(np.asarray(inputs["adj"]).T.reshape(PIECES, JT, P, PANELS, PW).transpose(3, 0, 2, 1, 4))
    x = np.ascontiguousarray(np.asarray(inputs["x"]).reshape(PANELS, KT, P, D).transpose(0, 2, 1, 3)
                             .reshape(PANELS, P, KT * D))
    arrays = {"at": at, "x_in": x}
    for short, name in (("w01", "L0_gnn_W1"), ("b01", "L0_gnn_b1"), ("w02", "L0_gnn_W2"), ("b02", "L0_gnn_b2"),
                        ("w11", "L1_gnn_W1"), ("b11", "L1_gnn_b1"), ("w12", "L1_gnn_W2"), ("b12", "L1_gnn_b2"),
                        ("w2", "L2_gnn_W"), ("w3", "L3_gnn_weight")):
        arrays[short] = np.ascontiguousarray(np.asarray(inputs[name]))
    args = [nc.dram_tensor(n, a.shape, mybir.dt.from_np(a.dtype), kind="ExternalInput").ap() for n, a in arrays.items()]
    out = nc.dram_tensor("out", [PANELS, P, KT * D], F32, kind="ExternalOutput").ap()
    build(nc, *args, out)
    r = run(nc, [arrays], core_ids=[0])
    got = np.asarray(r.results[0]["out"]).reshape(PANELS, P, KT, D).transpose(0, 2, 1, 3)
    return np.ascontiguousarray(got.reshape(N, D))
```

```python
import math

import numpy as np

import concourse.bass as bass
from concourse import mybir
from concourse.alu_op_type import AluOpType as ALU
from contextlib import ExitStack

F32 = mybir.dt.float32
F32R = mybir.dt.float32r
U32 = mybir.dt.uint32
ACT = mybir.ActivationFunctionType
AX = mybir.AxisListType

N, D, P = 4096, 128, 128
PANELS = 4
PW = N // PANELS
KT = PW // P
PIECES = 16
JT = N // P // PIECES
BANK = 512
CH = PW // BANK
RAW = 8
HI = 4
LN_EPS, L3_EPS, TOP = 1e-5, 1e-6, 4
CLIP, MIN_NORM, TINY = float(np.float32(1.0 - 1e-5)), 1e-15, 1e-10
ARTANH_CLIP = 0.5 * math.log((1.0 + CLIP) / (1.0 - CLIP))

SUMS, SMOOTH, KNN, GCN1, GCN2, HYPER, NORMED = range(7)
BUF = {SMOOTH: 0, KNN: 0, GCN1: 1, GCN2: 0, HYPER: 1, NORMED: 0}
ZBUF = 1
PER_X = PIECES // PANELS
EARLY = [(p * PIECES + t, p, (t + PER_X * p) % PIECES) for p in range(1, PANELS)
         for t in range(PIECES - PER_X * p, PIECES)]
LATE = ([(2, q) for q in range(8, 12)] + [(1, q) for q in range(4, 8)] + [(3, q) for q in range(12, 16)]
        + [(2, q) for q in range(12, 16)] + [(1, q) for q in range(8, 16)] + [(0, q) for q in range(16)])
SUMMED = PANELS * PIECES
SMOOTHED = EARLY + [(SUMMED + i, p, q) for i, (p, q) in enumerate(LATE)]
DONE_AT = {p: len(LATE) - 1 - [a for a, _ in LATE][::-1].index(p) for p in range(PANELS)}
assert sorted((p, q) for _, p, q in SMOOTHED) == [(p, q) for p in range(PANELS) for q in range(PIECES)]
assert len(LATE) % RAW == 0 and len(EARLY) % HI == 0
LATE_ENDS = [[(SUMS, 3, i)] if i < 8 else [] for i in range(12)] + [[(SMOOTH, 3, 2 * i), (SMOOTH, 3, 2 * i + 1)] for i in range(8)]\
    + [[(SMOOTH, 2, 2 * i), (SMOOTH, 2, 2 * i + 1)] for i in range(8)] + [[(SMOOTH, 1, i)] for i in range(12)]
assert len(LATE_ENDS) == len(LATE)
POOL_FIRST = [n % 4 != 3 if n < SUMMED else n % 4 == 3 for n, _, _ in SMOOTHED]
POOL_Q = {KNN: (), GCN1: (3, 7, 11, 15), GCN2: (3, 7, 11, 15),
          HYPER: (0, 2, 4, 6, 8, 10, 12, 14), NORMED: (3, 7, 11, 15)}
G_PE = (4, 6, 7, 9, 11, 12, 13)
G_DVE = tuple(q for q in range(PIECES) if q not in G_PE)
STREAMED = range(SMOOTH, NORMED + 1)
NEAR = -1


def build(nc, at, x, w01, b01, w02, b02, w11, b11, w12, b12, w2, w3, out):
    x_dram = {SUMS: x, NEAR: x, KNN: x, GCN2: nc.dram_tensor("x_after_0", [PANELS, P, KT * D], F32).ap(),
              HYPER: nc.dram_tensor("x_after_1", [PANELS, P, KT * D], F32).ap(),
              NORMED: nc.dram_tensor("x_after_2", [PANELS, P, KT * D], F32).ap()}
    scaled_rows = nc.dram_tensor("scaled_rows", [N, D], F32).ap()

    ctx = ExitStack()
    with ctx:
        def sem(name):
            return ctx.enter_context(nc.semaphore(name))

        arena_bytes = 211968
        ctx.enter_context(nc.sbuf_tensor("arena", [P, arena_bytes // 4], F32))
        base = nc.sbuf_base - arena_bytes
        top = [base]

        def at_byte(name, shape, dtype, offset):
            return nc.alloc_sbuf_tensor_at(name, [P, *shape], dtype, offset=offset)

        def place(name, shape, dtype):
            size = 4
            for s in shape:
                size *= s
            offset = top[0]
            top[0] += (size + 31) // 32 * 32
            assert top[0] <= base + arena_bytes, name
            return at_byte(name, shape, dtype, offset), offset

        raw, raw_at = place("raw", [RAW, JT, PW], F32)
        low = at_byte("low", [RAW, JT, PW], F32R, raw_at)
        high, high_at = place("high", [HI, JT, PW], F32R)
        scores = [at_byte(f"scores{i}", [N], F32, high_at + i * 4 * N) for i in range(2)]
        (xh0, _), (xh1, xh1_at) = [place(f"xh{i}", [N // P, D], F32R) for i in range(2)]
        xh = [xh0, xh1]
        a_sum = at_byte("a_sum", [2, JT, PW], F32, xh1_at)
        xl = [place(f"xl{i}", [N // P, D], F32R)[0] for i in range(2)]
        zh = xh[ZBUF][:, :, :].rearrange("p t d -> p (t d)")
        zl = xl[ZBUF][:, :, :].rearrange("p t d -> p (t d)")
        d_bc, d_at = place("d_bc", [N], F32)
        h_rows = at_byte("h_rows", [N], F32R, d_at)
        gathered = at_byte("gathered", [KT, TOP, D], F32, d_at)
        g_sum = at_byte("g_sum", [PW], F32, d_at)
        g_whole = at_byte("g_whole", [PW], F32, d_at + 4 * PW)
        t0, _ = place("t0", [PW], F32)
        t1, _ = place("t1", [PW], F32)
        t2, _ = place("t2", [PW], F32)
        xr, _ = place("xr", [PW], F32)
        w_names = ("w01", "w02", "w11", "w12", "w2", "w3")
        w = {n: place(n + "_sb", [D], F32)[0] for n in w_names}
        b02_bc, _ = place("b02_bc", [D], F32)
        b_cols, _ = place("b_cols", [3], F32)
        ident, _ = place("ident", [P], F32)
        ones, _ = place("ones", [P], F32)
        neg_half, _ = place("neg_half", [P], F32)
        ones_r, _ = place("ones_r", [P], F32R)
        z_tile_h = [place(f"z_tile_h{i}", [P], F32R)[0] for i in range(2)]
        z_tile_l = [place(f"z_tile_l{i}", [P], F32R)[0] for i in range(2)]
        top_v, _ = place("top_v", [KT, 8], F32)
        top_i, _ = place("top_i", [KT, 8], U32)
        near_i, _ = place("near_i", [N // P, TOP], U32)
        near_s, _ = place("near_s", [N // P, TOP], F32)
        ids, _ = place("ids", [KT, TOP], U32)
        dist, _ = place("dist", [KT, TOP], F32)
        a_rows, _ = place("a_rows", [N // P], F32)
        d_col, _ = place("d_col", [N // P], F32)
        s_col, _ = place("s_col", [N // P], F32)
        d2_col, _ = place("d2_col", [N // P], F32)
        sq_col, _ = place("sq_col", [N // P], F32)
        g_col, _ = place("g_col", [N // P], F32)
        g_parts, _ = place("g_parts", [2 * N // P + P], F32R)
        pick, _ = place("pick", [1], F32)
        stats, _ = place("stats", [KT, 6], F32)
        mv, _ = place("mv", [KT, 2], F32)
        c, _ = place("c", [16, KT], F32)

        ps = ctx.enter_context(nc.psum_tensor("ps", [P, 8 * BANK], F32))
        E0, E1 = 4 * BANK, 6 * BANK
        e0, e1 = ps[:, E0:E0 + PW], ps[:, E1:E1 + PW]

        def acc(p, lo=0, n=PW, s=None):
            if s == SMOOTH and p == 3:
                return ps[:, E0 + lo:E0 + lo + n]
            return ps[:, bass.ds(p % 2 * PW + lo, n)]

        def part(t, p, n=PW):
            return t[:, bass.ds(p * n, n)]

        def rows(t):
            return t.rearrange("p (t d) -> p t d", d=D)

        def tiles(t, p):
            return t[:, bass.ds(p * KT, KT), :]

        def g_place(p):
            return g_parts[:, bass.ds(p * (-2 * KT) + (PANELS - 1) * 2 * KT, 2 * KT)].rearrange("p (k i) -> p k i", i=2)

        def bc(t, n=D):
            return t.unsqueeze(2).to_broadcast([P, KT, n])

        loaded = [sem(f"loaded{i}") for i in range(RAW)]
        raw_free = sem("raw_free")
        hi_ready, lo_dve, lo_pool = sem("hi_ready"), sem("lo_dve"), sem("lo_pool")
        acc_free = sem("acc_free")
        consts_in, consts_up = sem("consts_in"), sem("consts_up")
        xr_in, xr_used = sem("xr_in"), sem("xr_used")
        stored = sem("stored")
        act_step = sem("act_step")
        S = {}

        def flag(name):
            if name not in S:
                S[name] = sem(name)
            return S[name]

        x_ready = {s: sem(f"x_ready{s}") for s in STREAMED}
        gathers = [sem(f"gathers{k}") for k in range(KT)]
        g_used = sem("g_used")
        x_stored = {s: sem(f"x_stored{s}") for s in (KNN, GCN2, HYPER, NORMED)}
        rows_stored = sem("rows_stored")

        def wait_apart(eng, which, value):
            eng.wait_ge(which, value)
            eng.sem_inc(flag("waited"), 1)

        class Chain:

            def __init__(self, eng, name, per):
                self.eng, self.sem, self.per = eng, flag(name), per

            def begin(self, p):
                self.p, self.k = p, 0

            def link(self, *ins, apart=False):
                for i in ins:
                    self.k += 1
                    i.then_inc(self.sem, 1)
                if apart:
                    wait_apart(self.eng, self.sem, self.per * self.p + self.k)
                else:
                    self.eng.wait_ge(self.sem, self.per * self.p + self.k)

            def end(self):
                assert self.k == self.per, (self.k, self.per)

        def weighed(p, q):
            return JT * (len(G_DVE) * p + sum(r <= q for r in G_DVE))

        def piece(s, p, q):
            return 16 * (4 * (s - SMOOTH) + p) + q

        def consumed(s, p, q):
            return RAW + len(LATE) + piece(s, p, q) + 1

        def slot_use(s, p, q):
            return 16 * (2 * (4 * (s - KNN) + p) + q // RAW + (SUMMED + len(LATE)) // RAW + 1)

        def low_count(s, p, q):
            mine = q in POOL_Q[s]
            n = POOL_FIRST.count(mine)
            n += sum(PANELS * (len(POOL_Q[r]) if mine else PIECES - len(POOL_Q[r])) for r in range(KNN, s))
            each = len(POOL_Q[s]) if mine else PIECES - len(POOL_Q[s])
            rank = sum((r in POOL_Q[s]) == mine for r in range(q + 1))
            return mine, n + each * p + rank

        def evictions(s, p):
            return 2 + 4 * (s - SMOOTH) + p + 1

        def smooth_ended(p):
            return PANELS - p

        XR_USERS = (SUMS, NEAR, KNN, GCN2, HYPER, NORMED)

        def xr_count(user, p):
            return 4 * XR_USERS.index(user) + p + 1

        block = ctx.enter_context(nc.Block())

        @block.sync
        def _(sp):
            sp.sem_inc(raw_free, RAW)
            in_turn = [(p, (t + PER_X * p) % PIECES) for p in range(PANELS) for t in range(PIECES)] + LATE
            for n, (p, q) in enumerate(in_turn):
                sp.wait_ge(raw_free, n + 1)
                sp.dma_start(raw[:, n % RAW, :, :], at[p, q]).then_inc(loaded[n % RAW], 16)
            with sp.Fori(0, NORMED - KNN + 1) as s:
                with sp.Fori(0, PANELS) as p:
                    for q in range(PIECES):
                        n = sp.snap((s * PANELS + p) * PIECES + (SUMMED + len(LATE) + q + 1))
                        sp.wait_ge(raw_free, n)
                        sp.dma_start(raw[:, q % RAW, :, :], at[bass.ds(p, 1), q].rearrange("o p j i -> (o p) j i"))\
                          .then_inc(loaded[q % RAW], 16)

        @block.gpsimd
        def _(pool):
            pool.memset(ident[:, :], 0.0).then_inc(consts_up, 1)
            pool.memset(ones[:, :], 1.0).then_inc(consts_up, 1)
            pool.memset(neg_half[:, :], -0.5).then_inc(consts_up, 1)
            pool.wait_ge(consts_up, 3)
            pool.affine_select(out=ident[:, :], in_=ident[:, :], compare_op=ALU.not_equal, fill=1.0,
                               base=0, pattern=[[-1, P]], channel_multiplier=1).then_inc(consts_up, 1)
            pool.tensor_copy(ones_r[:, :], ones[:, :]).then_inc(consts_up, 1)
            pool.sem_inc(flag("staging_free"), 2)
            pool.memset(g_parts[:, 2 * N // P:].bitcast(F32), 0.0).then_inc(flag("g_padded"), 1)
            pool.sem_inc(g_used, KT)

            def low_part(s, p, q):
                slot = q % RAW
                pool.wait_ge(hi_ready, piece(s, p, q) + 1)
                if s == HYPER and q in G_DVE:
                    pool.wait_ge(flag("g_sum_steps"), weighed(p, q))
                pool.tensor_tensor(low[:, slot], raw[:, slot], high[:, q % HI].bitcast(F32), ALU.subtract)\
                    .then_inc(lo_pool, 1)

            def finish(s, p, q):
                if s == NORMED and q == 1:
                    pool.wait_ge(xr_in, 16 * xr_count(NORMED, p))
                    pool.wait_ge(flag("normed_acc"), 1 + p)
                    pool.tensor_tensor(rows(t1[:, :]), rows(xr[:, :]), bc(part(s_col, p, KT)), ALU.mult)\
                        .then_inc(flag("normed_sx"), 1)

            def panel(s, p, done, dp):
                for q in range(PIECES):
                    if q in POOL_Q[s]:
                        low_part(s, p, q)
                    finish(done, dp, q)

            for m, (n, _, _) in enumerate(SMOOTHED):
                if POOL_FIRST[m]:
                    pool.wait_ge(hi_ready, m + 1)
                    if n < SUMMED:
                        pool.wait_ge(flag("sums_steps"), n + 1)
                    pool.tensor_tensor(low[:, n % RAW], raw[:, n % RAW], high[:, m % HI].bitcast(F32), ALU.subtract)\
                        .then_inc(lo_pool, 1)

            pool.wait_ge(flag("z_low"), PANELS)
            with pool.Fori(0, PANELS) as p:
                for k in range(KT):
                    pool.wait_ge(flag("staging_free"), KT * p + k + 1)
                    for src, dst in ((zh, z_tile_h), (zl, z_tile_l)):
                        pool.tensor_copy(dst[k % 2][:, :], src[:, bass.ds(p * PW + k * P, P)].bitcast(F32))\
                            .then_inc(flag("staged"), 1)

            pool.wait_ge(consts_in, 16 * 10)
            pool.wait_ge(rows_stored, 16 + 16 * PANELS)
            with pool.Fori(0, PANELS) as p:
                for k in range(KT):
                    pool.wait_ge(g_used, KT * p + k + 1)
                    pool.tensor_copy(ids[:, k, :], near_i[:, bass.ds(p * KT + k, 1), :].rearrange("p o k -> p (o k)"))\
                        .then_inc(flag("ids_up"), 1)
                    wait_apart(pool, flag("ids_up"), KT * p + k + 1)
                    for n in range(TOP):
                        pool.indirect_dma_start(
                            out=gathered[:, k, n, :], out_offset=None, in_=scaled_rows[:, :],
                            in_offset=bass.IndirectOffsetOnAxis(ap=ids[:, k, n:n + 1], axis=0),
                        ).then_inc(gathers[k], 16)
                pool.wait_ge(xr_in, 16 * xr_count(KNN, p))
                pool.tensor_tensor(rows(xr[:, :]), rows(xr[:, :]),
                                   b02_bc[:, :].unsqueeze(1).to_broadcast([P, KT, D]), ALU.add)\
                    .then_inc(flag("knn_xb"), 1)

            for s in range(GCN1, NORMED + 1):
                panel(s, 0, s - 1, 3)
                with pool.Fori(1, PANELS) as p:
                    panel(s, p, s, p - 1)
            for q in range(PIECES):
                finish(NORMED, 3, q)

        @block.scalar
        def _(act):
            for dst, src in ((w["w01"], w01), (w["w02"], w02), (w["w11"], w11), (w["w12"], w12), (w["w2"], w2),
                             (w["w3"], w3)):
                act.dma_start(dst[:, :], src).then_inc(consts_in, 16)
            act.dma_start(b02_bc[:, :], b02.partition_broadcast(P)).then_inc(consts_in, 16)
            for i, b in enumerate((b01, b11, b12)):
                act.dma_start(b_cols[:, i:i + 1], b.rearrange("(p o) -> p o", o=1)).then_inc(consts_in, 16)
            act.sem_inc(flag("scores_out"), 4)
            act.wait_ge(consts_in, 16 * 10)
            near_chain = Chain(act, "near_act", 1)

            def high_part(s, p, q):
                act.wait_ge(loaded[q % RAW], slot_use(s, p, q))
                act.wait_ge(raw_free, consumed(s, p, q) - HI)
                act.activation(high[:, q % HI], raw[:, q % RAW], ACT.Copy).then_inc(hi_ready, 1)

            def high_early(m):
                n = SMOOTHED[m][0]
                act.wait_ge(loaded[n % RAW], 16 * (n // RAW + 1))
                if m >= HI:
                    act.wait_ge(raw_free, RAW + SMOOTHED[m - HI][0] + 1)
                act.activation(high[:, m % HI], raw[:, n % RAW], ACT.Copy).then_inc(hi_ready, 1)

            def load_x(user, p):
                act.wait_ge(xr_used, xr_count(user, p))
                if user in (GCN2, HYPER, NORMED):
                    act.wait_ge(x_stored[{GCN2: KNN, HYPER: GCN2, NORMED: HYPER}[user]], 16 + 16 * PANELS)
                act.dma_start(xr[:, :], x_dram[user][bass.ds(p, 1)].rearrange("o p n -> (o p) n")).then_inc(xr_in, 16)

            def store_x(s, p):
                act.wait_ge(flag(f"y_up{s}"), p + 1)
                dst = out if s == NORMED else x_dram[{KNN: GCN2, GCN2: HYPER, HYPER: NORMED}[s]]
                act.dma_start(dst[bass.ds(p, 1)].rearrange("o p n -> (o p) n"), t2[:, :]).then_inc(x_stored[s], 16)

            def read_acc(p, func=ACT.Copy, **kw):
                act.activation(t0[:, :], acc(p), func, **kw).then_inc(acc_free, 1)

            def finish(s, p, q):
                if q == 0 and s in XR_USERS:
                    load_x(s, p)

                if s == SUMS:
                    if q == 1:
                        act.wait_ge(flag("sums_shifted"), p + 1)
                        act.activation(c[:, 0:2, :], c[:, 0:2, :], ACT.Sqrt).then_inc(flag("sums_roots"), 1)
                    if q == 3:
                        act.wait_ge(flag("sums_dx"), p + 1)
                        act.activation(tiles(xh[0], p), rows(t2[:, :]), ACT.Copy).then_inc(flag("sums_xh"), 1)
                    if q == 4:
                        act.wait_ge(flag("sums_d_bc"), p + 1)
                        act.activation(part(d_bc, p, PW), e1, ACT.Copy).then_inc(flag("d_bc_up"), 1)

                if s == SMOOTH:
                    if q == 5:
                        act.wait_ge(flag("smooth_w"), smooth_ended(p))
                        act.activation(t1[:, :], e0, ACT.Identity, bias=b_cols[:, 0:1]).then_inc(flag("smooth_b"), 1)
                    if q == 7:
                        act.wait_ge(flag("smooth_z"), smooth_ended(p))
                        act.activation(part(zh, p, PW), t1[:, :], ACT.Copy).then_inc(flag("z_high"), 1)
                        act.activation(t2[:, :], t1[:, :], ACT.Square).then_inc(flag("z_square"), 1)
                    if q == 10:
                        act.wait_ge(flag("z_norms"), smooth_ended(p))
                        act.activation(part(h_rows, p, PW), e1, ACT.Copy).then_inc(flag("h_high"), 1)
                        act.activation(part(sq_col, p, KT), ps[:, E0:E0 + KT], ACT.Copy).then_inc(flag("sq_col_up"), 1)

                if s == NEAR:
                    if q == 1:
                        near_chain.begin(p)
                        act.wait_ge(flag("near_d2"), p + 1)
                        near_chain.link(act.activation(dist[:, :, :], dist[:, :, :], ACT.Sqrt))
                        act.activation(tiles(near_s, p), dist[:, :, :], ACT.Exp, scale=-0.5)\
                            .then_inc(flag("near_s_up"), 1)
                        near_chain.end()
                    if q == 4:
                        act.wait_ge(flag("near_sums"), p + 1)
                        act.activation(c[:, 0, :], c[:, 0, :], ACT.Sqrt).then_inc(flag("near_roots"), 1)
                    if q == 7:
                        act.wait_ge(flag("near_dx"), p + 1)
                        act.activation(tiles(xh[0], p), rows(t0[:, :]), ACT.Copy).then_inc(flag("near_xh"), 1)
                        act.dma_start(scaled_rows[bass.ds(p * PW, PW), :].rearrange("(t p) d -> p t d", p=P),
                                      rows(t0[:, :])).then_inc(rows_stored, 16)

                if s == KNN:
                    if q == 5:
                        act.wait_ge(flag("knn_acc"), p + 1)
                        read_acc(p)
                    if q == 9:
                        root(s, p)
                    if q == 10:
                        rounded_x(s, p)
                        store_x(s, p)

                if s == GCN1:
                    if q == 1:
                        act.wait_ge(raw_free, consumed(s, p, PIECES - 1))
                        read_acc(p)
                    if q == 5:
                        act.wait_ge(flag("gcn1_w"), p + 1)
                        act.activation(t1[:, :], e0, ACT.Relu, bias=b_cols[:, 1:2]).then_inc(flag("gcn1_h"), 1)
                    if q == 9:
                        act.wait_ge(flag("gcn1_rows"), p + 1)
                        act.activation(tiles(xh[BUF[GCN2]], p), rows(e1), ACT.Copy).then_inc(flag("gcn1_xh"), 1)

                if s == GCN2:
                    if q == 1:
                        act.wait_ge(raw_free, consumed(s, p, PIECES - 1))
                        read_acc(p, ACT.Relu, bias=b_cols[:, 2:3])
                    if q == 5:
                        root(s, p)
                    if q == 6:
                        act.wait_ge(flag(f"y_up{s}"), p + 1)
                        store_x(s, p)
                        act.activation(t1[:, :], t2[:, :], ACT.Square).then_inc(flag("gcn2_x_sq"), 1)
                    if q == 7:
                        act.wait_ge(flag("gcn2_x_norm"), p + 1)
                        act.activation(c[:, 2, :], c[:, 0, :], ACT.Sqrt).then_inc(flag("gcn2_x_root"), 1)
                    if q == 8:
                        act.wait_ge(flag("gcn2_xt"), p + 1)
                        act.activation(t0[:, :], e0, ACT.Copy).then_inc(flag("gcn2_xt_read"), 1)
                        act.wait_ge(flag("gcn2_ratio"), p + 1)
                        act.activation(c[:, 5, :], c[:, 5, :], ACT.Ln).then_inc(flag("gcn2_ln"), 1)
                    if q == 10:
                        act.wait_ge(flag("gcn2_mx"), p + 1)
                        act.activation(t1[:, :], e0, ACT.Square).then_inc(flag("gcn2_mx_sq"), 1)
                    if q == 11:
                        act.wait_ge(flag("gcn2_mx_norm"), p + 1)
                        act.activation(c[:, 3, :], c[:, 1, :], ACT.Sqrt).then_inc(flag("gcn2_mx_root"), 1)
                    if q == 12:
                        act.wait_ge(flag("gcn2_arg"), p + 1)
                        act.activation(c[:, 5, :], c[:, 5, :], ACT.Tanh).then_inc(flag("gcn2_tanh"), 1)
                    if q == 13:
                        g_high = g_place(p)[:, :, 0]
                        act.wait_ge(flag("gcn2_g"), p + 1)
                        act.activation(g_high, part(g_col, p, KT), ACT.Copy)\
                           .then_inc(flag("gcn2_g_high"), 1)
                        rounded_x(s, p)

                if s == HYPER:
                    if q == 1:
                        act.wait_ge(raw_free, consumed(s, p, PIECES - 1))
                        read_acc(p)
                        act.activation(t1[:, :], e1, ACT.Copy).then_inc(flag("den_rows_up"), 1)
                    if q == 4:
                        act.wait_ge(flag("hyper_den"), 1 + p + 1)
                        act.activation(t1[:, :], e0, ACT.Square).then_inc(flag("hyper_sq"), 1)
                    if q == 5:
                        act.wait_ge(flag("hyper_norm"), p + 1)
                        act.activation(c[:, 0, :], c[:, 0, :], ACT.Sqrt).then_inc(flag("hyper_root"), 1)
                    if q == 6:
                        act.wait_ge(flag("hyper_ratio"), p + 1)
                        act.activation(c[:, 5, :], c[:, 5, :], ACT.Ln).then_inc(flag("hyper_ln"), 1)
                    if q == 7:
                        act.wait_ge(flag("hyper_u"), p + 1)
                        act.activation(t0[:, :], t1[:, :], ACT.Square).then_inc(flag("hyper_u_sq"), 1)
                    if q == 8:
                        act.wait_ge(flag("hyper_u_norm"), p + 1)
                        act.activation(c[:, 0, :], c[:, 0, :], ACT.Sqrt).then_inc(flag("hyper_u_root"), 1)
                    if q == 9:
                        act.wait_ge(flag("hyper_un"), p + 1)
                        act.activation(c[:, 1, :], c[:, 0, :], ACT.Tanh).then_inc(flag("hyper_u_tanh"), 1)
                    if q == 10:
                        root(s, p)
                    if q == 11:
                        store_x(s, p)
                        rounded_x(s, p)

                if s == NORMED:
                    if q == 4:
                        act.wait_ge(flag("normed_acc"), 1 + p + 1)
                        read_acc(p)
                    if q == 8:
                        root(s, p)
                    if q == 9:
                        store_x(s, p)

            def root(s, p):
                act.wait_ge(flag(f"var_up{s}"), p + 1)
                act.activation(c[:, 14, :], c[:, 14, :], ACT.Sqrt).then_inc(flag(f"root_up{s}"), 1)

            def rounded_x(s, p):
                src = {KNN: t2, GCN2: t1, HYPER: t0}[s]
                act.wait_ge(flag(f"new_x{s}"), p + 1)
                act.activation(tiles(xh[BUF[s + 1]], p), rows(src[:, :]), ACT.Copy).then_inc(flag(f"new_xh{s}"), 1)

            def panel(s, p, done, dp):
                for q in range(PIECES):
                    high_part(s, p, q)
                    finish(done, dp, q)

            streamed_as = {n: m for m, (n, _, _) in enumerate(SMOOTHED)}
            for p in range(1, PANELS):
                for t in range(PIECES):
                    if PIECES * p + t in streamed_as:
                        high_early(streamed_as[PIECES * p + t])
                    finish(SUMS, p - 1, t - 4)
            for i, ends in enumerate(LATE_ENDS):
                high_early(len(EARLY) + i)
                for end in ends:
                    finish(*end)
            for q in range(PIECES):
                finish(SMOOTH, 0, q)

            def scores_out(p, q):
                k = q // 2
                if q % 2 == 0:
                    act.wait_ge(flag("searched"), KT * p + k + 1)
                for r in range(2):
                    pair = q % 2 * 2 + r
                    act.wait_ge(flag("scores_up"), 4 * (KT * p + k) + pair + 1)
                    act.activation(scores[k % 2][:, pair * PW:(pair + 1) * PW], ps[:, pair * PW:(pair + 1) * PW],
                                   ACT.Copy).then_inc(flag("scores_out"), 1)

            for q in range(PIECES):
                scores_out(0, q)
            with act.Fori(1, PANELS) as p:
                for q in range(PIECES):
                    scores_out(p, q)
                    finish(NEAR, p - 1, q)

            act.wait_ge(flag("searched"), 2 + N // P)
            panel(KNN, 0, NEAR, 3)
            with act.Fori(1, PANELS) as p:
                panel(KNN, p, KNN, p - 1)
            for s in range(GCN1, NORMED + 1):
                panel(s, 0, s - 1, 3)
                with act.Fori(1, PANELS) as p:
                    panel(s, p, s, p - 1)
            for q in range(PIECES):
                finish(NORMED, 3, q)
            act.wait_ge(x_stored[NORMED], 16 + 16 * PANELS)

        @block.vector
        def _(dve):
            TT, TS, STT = dve.tensor_tensor, dve.tensor_scalar, dve.scalar_tensor_tensor
            near = Chain(dve, "near_dve", 3)
            picks = Chain(dve, "picks_dve", TOP * KT)
            ln = {s: Chain(dve, f"norm_dve{s}", n) for s, n in
                  ((KNN, 2 + 2 * KT + 1), (GCN2, 2 * KT + 1), (HYPER, 2 * KT + 1), (NORMED, 2 + 2 * KT + 1))}
            mob = Chain(dve, "mobius_dve", 17)
            hyp = Chain(dve, "hyper_dve", 23)
            dve.sem_inc(flag("searched"), 2)
            dve.sem_inc(acc_free, 2)
            for which in (xr_used, *(flag(n) for n in ("normed_acc", "g_whole_up", "hyper_den", "den_rows_up", "sums_read"))):
                dve.sem_inc(which, 1)
            for which in (rows_stored, *x_stored.values()):
                dve.sem_inc(which, 16)
            dve.wait_ge(consts_up, 5)
            TT(pick[:, :], ident[:, 0:1], ident[:, 1:2], ALU.add).then_inc(consts_up, 1)

            def add_piece(p, q):
                n = PIECES * p + q
                dve.wait_ge(loaded[n % RAW], 16 * (n // RAW + 1))
                if q == 0:
                    if p > 1:
                        dve.wait_ge(flag("sums_read"), p)
                    ins = dve.tensor_copy(a_sum[:, p % 2], raw[:, 0])
                else:
                    dve.wait_ge(flag("sums_steps"), n)
                    ins = TT(a_sum[:, p % 2], a_sum[:, p % 2], raw[:, q % RAW], ALU.add)
                ins.then_inc(flag("sums_steps"), 1)

            def low_early(m):
                n = SMOOTHED[m][0]
                dve.wait_ge(hi_ready, m + 1)
                if n < SUMMED:
                    dve.wait_ge(flag("sums_steps"), n + 1)
                TT(low[:, n % RAW], raw[:, n % RAW], high[:, m % HI].bitcast(F32), ALU.subtract).then_inc(lo_dve, 1)

            def low_part(s, p, q):
                slot = q % RAW
                dve.wait_ge(hi_ready, piece(s, p, q) + 1)
                if s == HYPER and q in G_DVE:
                    dve.wait_ge(flag("g_sum_steps"), weighed(p, q))
                TT(low[:, slot], raw[:, slot], high[:, q % HI].bitcast(F32), ALU.subtract).then_inc(lo_dve, 1)

            def weigh_piece(p, q):
                dve.wait_ge(hi_ready, piece(HYPER, p, q) + 1)
                for j in range(JT):
                    n = JT * q + j
                    if n == 0:
                        dve.wait_ge(flag("g_whole_up"), 1 + p)
                        ins = TS(g_sum[:, :], raw[:, 0, 0], g_col[:, 0:1], None, ALU.mult)
                    else:
                        dve.wait_ge(flag("g_sum_steps"), weighed(p, q) - JT + j)
                        ins = STT(g_sum[:, :], raw[:, q % RAW, j], g_col[:, n:n + 1], g_sum[:, :], ALU.mult, ALU.add)
                    ins.then_inc(flag("g_sum_steps"), 1)
                if q == G_DVE[-1]:
                    dve.wait_ge(flag("g_sum_steps"), weighed(p, q))
                    dve.wait_ge(flag("hyper_den"), 1 + p)
                    dve.tensor_copy(g_whole[:, :], g_sum[:, :]).then_inc(flag("g_whole_up"), 1)

            def variances(s, p, src):
                ch = ln[s]
                ch.link(*[dve.bn_stats(stats[:, k, :], rows(src[:, :])[:, k, :]) for k in range(KT)], apart=True)
                ch.link(*[dve.bn_aggr(mv[:, k, :], stats[:, k, :]) for k in range(KT)])
                TS(c[:, 14, :], mv[:, :, 1], LN_EPS, None, ALU.add).then_inc(flag(f"var_up{s}"), 1)

            def normalise(s, p, src):
                ch = ln[s]
                dve.wait_ge(flag(f"root_up{s}"), p + 1)
                ch.link(dve.reciprocal(c[:, 15, :], c[:, 14, :]))
                ch.end()
                dve.wait_ge(x_stored[s], 16 + 16 * p)
                if s == KNN:
                    dve.wait_ge(flag("knn_acc"), p + 1)
                for k in range(KT):
                    last = TS(rows(t2[:, :])[:, k, :], rows(src[:, :])[:, k, :], mv[:, k, 0:1], c[:, 15, k:k + 1],
                              ALU.subtract, ALU.mult)
                    if k < KT - 1:
                        last.then_inc(flag(f"y_part{s}"), 1)
                dve.wait_ge(flag(f"y_part{s}"), (KT - 1) * (p + 1))
                last.then_inc(flag(f"y_up{s}"), 1)

            def rest_of_x(s, p, src):
                dve.wait_ge(flag(f"new_xh{s}"), p + 1)
                TT(tiles(xl[BUF[s + 1]], p), rows(src[:, :]), tiles(xh[BUF[s + 1]], p).bitcast(F32), ALU.subtract)\
                    .then_inc(x_ready[s + 1], 1)
                dve.wait_ge(x_ready[s + 1], p + 1)

            def ratio(chain, src, lo, hi):
                chain.link(TS(c[:, lo, :], c[:, src, :], CLIP, None, ALU.min))
                chain.link(TS(c[:, hi, :], c[:, lo, :], 1.0, None, ALU.add),
                           TS(c[:, lo + 1, :], c[:, lo, :], -1.0, 1.0, ALU.mult, ALU.add))
                chain.link(dve.reciprocal(c[:, lo + 1, :], c[:, lo + 1, :]))
                return TT(c[:, hi, :], c[:, hi, :], c[:, lo + 1, :], ALU.mult)

            def finish(s, p, q):
                if s == SUMS:
                    if q == 0:
                        dve.wait_ge(flag("sums_read"), 1 + p + 1)
                        dve.tensor_copy(part(a_rows, p, KT), ps[:, E1:E1 + KT]).then_inc(flag("a_rows_up"), 1)
                        dve.tensor_copy(c[:, 0, :], ps[:, E1:E1 + KT]).then_inc(flag("a_rows_up"), 1)
                        TS(c[:, 1, :], ps[:, E1:E1 + KT], L3_EPS, None, ALU.add).then_inc(flag("sums_shifted"), 1)
                    if q == 2:
                        dve.wait_ge(flag("sums_roots"), p + 1)
                        dve.reciprocal(part(s_col, p, KT), c[:, 1, :]).then_inc(flag("s_col_up"), 1)
                        dve.reciprocal(part(d_col, p, KT), c[:, 0, :]).then_inc(flag("d_col_up"), 1)
                        dve.wait_ge(flag("d_col_up"), p + 1)
                        dve.wait_ge(xr_in, 16 * xr_count(SUMS, p))
                        TT(rows(t2[:, :]), rows(xr[:, :]), bc(part(d_col, p, KT)), ALU.mult).then_inc(flag("sums_dx"), 1)
                    if q == 3:
                        dve.wait_ge(flag("sums_xh"), p + 1)
                        TT(tiles(xl[0], p), rows(t2[:, :]), tiles(xh[0], p).bitcast(F32), ALU.subtract)\
                            .then_inc(x_ready[SMOOTH], 1)
                        dve.wait_ge(x_ready[SMOOTH], p + 1)
                        TT(rows(xr[:, :]), ident[:, :].unsqueeze(1).to_broadcast([P, KT, P]),
                           bc(part(d_col, p, KT), P), ALU.mult).then_inc(flag("sums_diag"), 1)

                if s == SMOOTH:
                    if q == 1:
                        dve.wait_ge(raw_free, RAW + SUMMED + DONE_AT[p] + 1)
                        dve.wait_ge(flag("d_bc_up"), PANELS)
                        TT(t0[:, :], acc(p, s=SMOOTH), part(d_bc, p, PW), ALU.mult).then_inc(acc_free, 1)
                    if q == 6:
                        dve.wait_ge(flag("smooth_b"), smooth_ended(p))
                        STT(t1[:, :], t1[:, :], 0.1, t1[:, :], ALU.mult, ALU.max).then_inc(flag("smooth_z"), 1)
                    if q == 8:
                        dve.wait_ge(flag("z_high"), smooth_ended(p))
                        TT(part(zl, p, PW), t1[:, :], part(zh, p, PW).bitcast(F32), ALU.subtract)\
                            .then_inc(flag("z_low"), 1)
                    if q == 11:
                        dve.wait_ge(flag("h_high"), smooth_ended(p))
                        h = part(h_rows, p, PW)
                        TT(t2[:, :], e1, h.bitcast(F32), ALU.subtract).then_inc(flag("h_low"), 1)
                        dve.wait_ge(flag("h_low"), 2 * smooth_ended(p) - 1)
                        TS(t2[:, :], t2[:, :], ident[:, 1:2], None, ALU.mult).then_inc(flag("h_low"), 1)
                        dve.wait_ge(flag("h_low"), 2 * smooth_ended(p))
                        STT(h, h.bitcast(F32), ident[:, 0:1], t2[:, :], ALU.mult, ALU.add).then_inc(flag("h_up"), 1)

                if s == NEAR:
                    if q == 0:
                        near.begin(p)
                        dve.wait_ge(flag("sq_col_up"), PANELS)
                        near.link(STT(dist[:, :, :], top_v[:, :, 0:TOP], -2.0, bc(part(sq_col, p, KT), TOP),
                                      ALU.mult, ALU.add))
                        TS(dist[:, :, :], dist[:, :, :], 0.0, TINY, ALU.max, ALU.add).then_inc(flag("near_d2"), 1)
                        near.link(dve.tensor_copy(tiles(near_i, p), top_i[:, :, 0:TOP]))
                    if q == 3:
                        dve.wait_ge(flag("near_s_up"), p + 1)
                        near.link(dve.tensor_reduce(out=c[:, 1, :], in_=tiles(near_s, p), op=ALU.add, axis=AX.X))
                        near.end()
                        TT(c[:, 0, :], c[:, 1, :], part(a_rows, p, KT), ALU.add).then_inc(flag("near_sums"), 1)
                    if q == 6:
                        dve.wait_ge(flag("near_roots"), p + 1)
                        dve.reciprocal(part(d2_col, p, KT), c[:, 0, :]).then_inc(flag("d2_col_up"), 1)
                        dve.wait_ge(flag("d2_col_up"), p + 1)
                        dve.wait_ge(xr_in, 16 * xr_count(NEAR, p))
                        dve.wait_ge(rows_stored, 16 + 16 * p)
                        TT(rows(t0[:, :]), rows(xr[:, :]), bc(part(d2_col, p, KT)), ALU.mult)\
                            .then_inc(flag("near_dx"), 1)
                    if q == 8:
                        dve.wait_ge(flag("near_xh"), p + 1)
                        TT(tiles(xl[0], p), rows(t0[:, :]), tiles(xh[0], p).bitcast(F32), ALU.subtract)\
                            .then_inc(x_ready[KNN], 1)
                        dve.wait_ge(x_ready[KNN], p + 1)
                        dve.sem_inc(xr_used, 1)

                if s == KNN:
                    if q == 0:
                        picks.begin(p)
                    for k in range(2 * q, min(2 * q + 2, KT)):
                        dve.wait_ge(gathers[k], 16 * TOP * (p + 1))
                        y = rows(t2[:, :])[:, k, :]
                        if k == 0:
                            dve.wait_ge(x_stored[KNN], 16 + 16 * p)
                        for n in range(TOP):
                            weight = near_s[:, bass.ds(p * KT + k, 1), n:n + 1].rearrange("p o k -> p (o k)")
                            if n == 0:
                                picks.link(TS(y, gathered[:, k, 0, :], weight, None, ALU.mult))
                            else:
                                picks.link(STT(y, gathered[:, k, n, :], weight, y, ALU.mult, ALU.add))
                        dve.sem_inc(g_used, 1)
                        if k == KT - 1:
                            picks.end()
                            dve.sem_inc(flag("picked"), 1)
                    if q == 8:
                        dve.wait_ge(flag("knn_rows"), p + 1)
                        dve.wait_ge(flag("knn_xb"), p + 1)
                        ch = ln[s]
                        ch.begin(p)
                        ch.link(TT(rows(t1[:, :]), rows(e0), bc(part(d2_col, p, KT)), ALU.mult))
                        ch.link(TT(t1[:, :], t1[:, :], xr[:, :], ALU.add))
                        dve.sem_inc(xr_used, 1)
                        variances(s, p, t1)
                    if q == 9:
                        normalise(s, p, t1)
                        dve.wait_ge(flag(f"y_up{s}"), p + 1)
                        dve.sem_inc(flag(f"new_x{s}"), 1)
                    if q == 10:
                        rest_of_x(s, p, t2)

                if s == GCN1:
                    if q == 10:
                        dve.wait_ge(flag("gcn1_xh"), p + 1)
                        TT(tiles(xl[BUF[GCN2]], p), rows(e1), tiles(xh[BUF[GCN2]], p).bitcast(F32), ALU.subtract)\
                            .then_inc(x_ready[GCN2], 1)

                if s == GCN2:
                    if q == 4:
                        dve.wait_ge(flag("gcn2_rows"), p + 1)
                        dve.wait_ge(xr_in, 16 * xr_count(s, p))
                        ln[s].begin(p)
                        TT(t1[:, :], e0, xr[:, :], ALU.add).then_inc(xr_used, 1)
                        dve.wait_ge(xr_used, 1 + xr_count(s, p))
                        variances(s, p, t1)
                    if q == 5:
                        normalise(s, p, t1)
                    if q == 6:
                        dve.wait_ge(flag("gcn2_x_sq"), p + 1)
                        dve.tensor_reduce(out=c[:, 0, :], in_=rows(t1[:, :]), op=ALU.add, axis=AX.X)\
                           .then_inc(flag("gcn2_x_norm"), 1)
                    if q == 7:
                        mob.begin(p)
                        dve.wait_ge(flag("gcn2_x_root"), p + 1)
                        mob.link(TS(c[:, 2, :], c[:, 2, :], MIN_NORM, None, ALU.max))
                        ratio(mob, 2, 8, 5).then_inc(flag("gcn2_ratio"), 1)
                        mob.link(dve.reciprocal(c[:, 6, :], c[:, 2, :]))
                    if q == 8:
                        dve.wait_ge(flag("gcn2_ln"), p + 1)
                        mob.link(STT(c[:, 6, :], c[:, 5, :], 0.5, c[:, 6, :], ALU.mult, ALU.mult))
                    if q == 10:
                        dve.wait_ge(flag("gcn2_mx_sq"), p + 1)
                        dve.tensor_reduce(out=c[:, 1, :], in_=rows(t1[:, :]), op=ALU.add, axis=AX.X)\
                           .then_inc(flag("gcn2_mx_norm"), 1)
                    if q == 11:
                        dve.wait_ge(flag("gcn2_mx_root"), p + 1)
                        mob.link(TS(c[:, 3, :], c[:, 3, :], MIN_NORM, None, ALU.max))
                        TT(c[:, 5, :], c[:, 3, :], c[:, 6, :], ALU.mult).then_inc(flag("gcn2_arg"), 1)
                        mob.link(dve.reciprocal(c[:, 7, :], c[:, 3, :]))
                    if q == 12:
                        dve.wait_ge(flag("gcn2_tanh"), p + 1)
                        mob.link(TT(c[:, 5, :], c[:, 5, :], c[:, 7, :], ALU.mult))
                        mob.link(TT(c[:, 10, :], c[:, 1, :], c[:, 5, :], ALU.mult))
                        mob.link(TT(c[:, 10, :], c[:, 10, :], c[:, 5, :], ALU.mult))
                        mob.link(TS(c[:, 10, :], c[:, 10, :], -1.0, 1.0, ALU.mult, ALU.add))
                        mob.link(TS(c[:, 10, :], c[:, 10, :], 1e-5, None, ALU.max))
                        mob.link(dve.reciprocal(c[:, 10, :], c[:, 10, :]))
                        mob.link(TS(c[:, 10, :], c[:, 10, :], 2.0, None, ALU.mult))
                        TS(part(g_col, p, KT), c[:, 10, :], -1.0, None, ALU.add).then_inc(flag("gcn2_g"), 1)
                        mob.link(TT(c[:, 10, :], c[:, 10, :], c[:, 5, :], ALU.mult))
                        mob.end()
                        TT(rows(t1[:, :]), rows(e0), bc(c[:, 10, :]), ALU.mult).then_inc(flag(f"new_x{s}"), 1)
                    if q == 13:
                        spot = g_place(p)
                        g_high, g_low = spot[:, :, 0], spot[:, :, 1]
                        dve.wait_ge(flag("gcn2_g_high"), p + 1)
                        TT(g_low, part(g_col, p, KT), g_high.bitcast(F32), ALU.subtract).then_inc(flag("gcn2_g_low"), 1)
                        dve.wait_ge(flag("gcn2_g_low"), p + 1)
                        rest_of_x(s, p, t1)

                if s == HYPER:
                    if q == 4:
                        hyp.begin(p)
                        den = acc(p, 0, KT)
                        dve.wait_ge(flag("hyper_den"), 1 + p + 1)
                        hyp.link(TS(c[:, 2, :], den, TINY, None, ALU.max), TS(c[:, 3, :], den, -TINY, None, ALU.min),
                                 TS(c[:, 4, :], den, 0.0, None, ALU.is_ge))
                        hyp.link(TT(c[:, 2, :], c[:, 2, :], c[:, 3, :], ALU.subtract))
                        hyp.link(TT(c[:, 2, :], c[:, 2, :], c[:, 4, :], ALU.mult))
                        hyp.link(TT(c[:, 2, :], c[:, 2, :], c[:, 3, :], ALU.add))
                        hyp.link(dve.reciprocal(c[:, 2, :], c[:, 2, :]))
                        dve.wait_ge(flag("hyper_sq"), p + 1)
                        dve.tensor_reduce(out=c[:, 0, :], in_=rows(t1[:, :]), op=ALU.add, axis=AX.X)\
                           .then_inc(flag("hyper_norm"), 1)
                    if q == 5:
                        dve.wait_ge(flag("hyper_root"), p + 1)
                        hyp.link(TT(c[:, 1, :], c[:, 0, :], c[:, 2, :], ALU.mult))
                        hyp.link(STT(c[:, 1, :], c[:, 1, :], -1.0, c[:, 1, :], ALU.mult, ALU.max))
                        hyp.link(TS(c[:, 1, :], c[:, 1, :], MIN_NORM, None, ALU.max))
                        ratio(hyp, 1, 8, 5).then_inc(flag("hyper_ratio"), 1)
                        hyp.link(dve.reciprocal(c[:, 7, :], c[:, 1, :]))
                        hyp.link(TT(c[:, 2, :], c[:, 2, :], c[:, 7, :], ALU.mult))
                    if q == 6:
                        dve.wait_ge(flag("hyper_ln"), p + 1)
                        hyp.link(STT(c[:, 5, :], c[:, 5, :], 0.25, part(a_rows, p, KT), ALU.mult, ALU.mult))
                        hyp.link(TS(c[:, 5, :], c[:, 5, :], ARTANH_CLIP, -ARTANH_CLIP, ALU.min, ALU.max))
                        hyp.link(TT(c[:, 2, :], c[:, 2, :], c[:, 5, :], ALU.mult))
                        hyp.link(TT(rows(t1[:, :]), rows(e0), bc(c[:, 2, :]), ALU.mult))
                        TS(t1[:, :], t1[:, :], 0.0, None, ALU.max).then_inc(flag("hyper_u"), 1)
                    if q == 7:
                        dve.wait_ge(flag("hyper_u_sq"), p + 1)
                        dve.tensor_reduce(out=c[:, 0, :], in_=rows(t0[:, :]), op=ALU.add, axis=AX.X)\
                           .then_inc(flag("hyper_u_norm"), 1)
                    if q == 8:
                        dve.wait_ge(flag("hyper_u_root"), p + 1)
                        TS(c[:, 0, :], c[:, 0, :], MIN_NORM, None, ALU.max).then_inc(flag("hyper_un"), 1)
                        dve.wait_ge(flag("hyper_un"), p + 1)
                        hyp.link(dve.reciprocal(c[:, 3, :], c[:, 0, :]))
                    if q == 9:
                        dve.wait_ge(flag("hyper_u_tanh"), p + 1)
                        hyp.link(TT(c[:, 3, :], c[:, 3, :], c[:, 1, :], ALU.mult))
                        hyp.link(TT(rows(t1[:, :]), rows(t1[:, :]), bc(c[:, 3, :]), ALU.mult))
                        hyp.end()
                        dve.wait_ge(xr_in, 16 * xr_count(s, p))
                        TT(t1[:, :], t1[:, :], xr[:, :], ALU.add).then_inc(xr_used, 1)
                        dve.wait_ge(xr_used, 1 + xr_count(s, p))
                        ln[s].begin(p)
                        variances(s, p, t1)
                    if q == 10:
                        normalise(s, p, t1)
                        dve.wait_ge(flag(f"y_up{s}"), p + 1)
                        TT(rows(t0[:, :]), rows(t2[:, :]), bc(part(s_col, p, KT)), ALU.mult)\
                            .then_inc(flag(f"new_x{s}"), 1)
                    if q == 11:
                        rest_of_x(s, p, t0)

                if s == NORMED:
                    if q == 7:
                        dve.wait_ge(flag("normed_rows"), p + 1)
                        ch = ln[s]
                        ch.begin(p)
                        ch.link(TT(rows(t1[:, :]), rows(e0), bc(part(s_col, p, KT)), ALU.mult))
                        ch.link(TT(t1[:, :], t1[:, :], xr[:, :], ALU.add))
                        dve.sem_inc(xr_used, 1)
                        variances(s, p, t1)
                    if q == 8:
                        normalise(s, p, t1)

            def panel(s, p, done, dp):
                for q in range(PIECES):
                    if s == HYPER and q in G_DVE:
                        weigh_piece(p, q)
                    if q not in POOL_Q[s]:
                        low_part(s, p, q)
                    finish(done, dp, q)

            streamed_as = {n: m for m, (n, _, _) in enumerate(SMOOTHED)}
            for p in range(PANELS):
                for t in range(PIECES):
                    add_piece(p, t)
                    m = streamed_as.get(PIECES * p + t)
                    if m is not None and not POOL_FIRST[m]:
                        low_early(m)
                    if p > 0:
                        finish(SUMS, p - 1, t - 4)
            for i, ends in enumerate(LATE_ENDS):
                if not POOL_FIRST[len(EARLY) + i]:
                    low_early(len(EARLY) + i)
                for end in ends:
                    finish(*end)
            for q in range(PIECES):
                finish(SMOOTH, 0, q)

            def search(p, k):
                wait_apart(dve, flag("scores_out"), 4 + 4 * (KT * p + k + 1))
                dve.max(out=top_v[:, k, :], in_=scores[k % 2][:, :]).then_inc(flag("maxima"), 1)
                wait_apart(dve, flag("maxima"), KT * p + k + 1)
                dve.max_index(out=top_i[:, k, :], in_max=top_v[:, k, :], in_values=scores[k % 2][:, :])\
                   .then_inc(flag("searched"), 1)

            for k in range(KT):
                search(0, k)
            with dve.Fori(1, PANELS) as p:
                dve.wait_ge(flag("searched"), 2 + KT * p)
                finish(NEAR, p - 1, 0)
                for k in range(KT):
                    search(p, k)
                    for q in (2 * k + 1, 2 * k + 2):
                        finish(NEAR, p - 1, q)
            dve.wait_ge(flag("searched"), 2 + N // P)
            panel(KNN, 0, NEAR, 3)
            with dve.Fori(1, PANELS) as p:
                panel(KNN, p, KNN, p - 1)
            for s in range(GCN1, NORMED + 1):
                panel(s, 0, s - 1, 3)
                with dve.Fori(1, PANELS) as p:
                    panel(s, p, s, p - 1)
            for q in range(PIECES):
                finish(NORMED, 3, q)

        @block.tensor
        def _(pe):
            mm = pe.matmul

            def chunk(t, i):
                return t[:, i * BANK:(i + 1) * BANK]

            def by_weights(name, src, weights):
                for i in range(CH):
                    last = mm(chunk(e0, i), weights[:, :], chunk(src, i), start=True, stop=True)
                last.then_inc(flag(name), 1)

            def by_tiles(name, dst, src, right):
                for k in range(KT):
                    last = mm(dst[:, k * D:(k + 1) * D], src[:, k * P:(k + 1) * P], right[:, :], start=True, stop=True)
                last.then_inc(flag(name), 1)

            def turned(name, dst, src):
                for k in range(KT):
                    last = pe.transpose(dst[:, k * D:(k + 1) * D], src[:, k * P:(k + 1) * P], ident[:, :])
                last.then_inc(flag(name), 1)

            def sums_down(name, col, *srcs):
                for k in range(KT):
                    for i, src in enumerate(srcs):
                        last = mm(ps[:, col + k:col + k + 1], src[:, k * P:(k + 1) * P], ones[:, 0:1],
                                  start=i == 0, stop=i == len(srcs) - 1)
                last.then_inc(flag(name), 1)

            def add_turned(name, p, src):
                for k in range(KT):
                    last = mm(acc(p, k * P, P), src[:, k * P:(k + 1) * P], ident[:, :], start=False,
                              stop=k % (BANK // P) == BANK // P - 1)
                last.then_inc(flag(name), 1)

            def weigh(q, a, first=False, last=False):
                for j in range(JT):
                    n = JT * q + j
                    at_col = 2 * ((PANELS - 1 - n // KT) * KT + n % KT)
                    factors = g_parts[:, at_col:at_col + P]
                    for i in range(CH):
                        mm(chunk(e1, i), factors, chunk(a[:, j], i), start=first and j == 0,
                           stop=last and j == JT - 1)

            def product(s, p, q):
                b, slot, stays = BUF[s], q % RAW, s in (KNN, NORMED)
                if q == 0:
                    pe.wait_ge(acc_free, evictions(s, p) - 2)
                if q % 4 == 0 and isinstance(p, int):
                    pe.wait_ge(x_ready[s], q // 4 + 1)
                pe.wait_ge(hi_ready, piece(s, p, q) + 1)
                for j in range(JT):
                    for x_part in (xh[b], xl[b]):
                        for i in range(CH):
                            mm(acc(p, i * BANK, BANK), x_part[:, JT * q + j, :], chunk(high[:, q % HI, j], i),
                               start=(q, j) == (0, 0) and x_part is xh[b], stop=False)
                if s == HYPER and q in G_PE:
                    if q == G_PE[0]:
                        pe.wait_ge(flag("g_padded"), 1)
                        pe.wait_ge(flag("den_rows_up"), 1 + p)
                    weigh(q, high[:, q % HI], first=q == G_PE[0])
                by_pool, count = low_count(s, p, q)
                pe.wait_ge(lo_pool if by_pool else lo_dve, count)
                if s == HYPER and q in G_PE:
                    weigh(q, low[:, slot], last=q == G_PE[-1])
                for j in range(JT):
                    for i in range(CH):
                        last = mm(acc(p, i * BANK, BANK), xh[b][:, JT * q + j, :], chunk(low[:, slot, j], i),
                                  start=False, stop=(q, j) == (PIECES - 1, JT - 1) and not stays)
                last.then_inc(raw_free, 1)

            def product_early(m):
                n, p, q = SMOOTHED[m]
                if n == SUMMED + LATE.index((0, 0)):
                    pe.wait_ge(acc_free, 2 + smooth_ended(2))
                pe.wait_ge(x_ready[SMOOTH], q // PER_X + 1)
                pe.wait_ge(hi_ready, m + 1)
                for j in range(JT):
                    for x_part in (xh[BUF[SMOOTH]], xl[BUF[SMOOTH]]):
                        for i in range(CH):
                            mm(acc(p, i * BANK, BANK, SMOOTH), x_part[:, JT * q + j, :], chunk(high[:, m % HI, j], i),
                               start=(q, j) == (0, 0) and x_part is xh[BUF[SMOOTH]], stop=False)
                pe.wait_ge(lo_pool if POOL_FIRST[m] else lo_dve, POOL_FIRST[:m + 1].count(POOL_FIRST[m]))
                for j in range(JT):
                    for i in range(CH):
                        last = mm(acc(p, i * BANK, BANK, SMOOTH), xh[BUF[SMOOTH]][:, JT * q + j, :],
                                  chunk(low[:, n % RAW, j], i), start=False, stop=(q, j) == (PIECES - 1, JT - 1))
                last.then_inc(raw_free, 1)

            def finish(s, p, q):
                if s == SUMS:
                    if q == 4:
                        pe.wait_ge(flag("sums_diag"), p + 1)
                        for i in range(CH):
                            last = mm(chunk(e1, i), ones[:, :], chunk(xr, i), start=True, stop=True)
                        last.then_inc(flag("sums_d_bc"), 1)
                        pe.wait_ge(flag("sums_d_bc"), p + 1)
                        pe.sem_inc(xr_used, 1)
                if s == SMOOTH:
                    if q == 3:
                        pe.wait_ge(acc_free, 2 + smooth_ended(p))
                        by_weights("smooth_w", t0, w["w01"])
                    if q == 9:
                        pe.wait_ge(flag("z_square"), smooth_ended(p))
                        for i in range(CH):
                            mm(chunk(e1, i), neg_half[:, :], chunk(t2, i), start=True, stop=True)
                        sums_down("z_norms", E0, t2)
                if s == KNN:
                    if q == 4:
                        pe.wait_ge(flag("picked"), p + 1)
                        add_turned("knn_acc", p, t2)
                    if q == 6:
                        pe.wait_ge(acc_free, evictions(s, p))
                        by_tiles("knn_rows", e0, t0, w["w02"])
                if s == GCN1:
                    if q == 3:
                        pe.wait_ge(acc_free, evictions(s, p))
                        by_weights("gcn1_w", t0, w["w11"])
                    if q == 7:
                        pe.wait_ge(flag("gcn1_h"), p + 1)
                        by_tiles("gcn1_rows", e1, t1, w["w12"])
                if s == GCN2:
                    if q == 2:
                        pe.wait_ge(acc_free, evictions(s, p))
                        turned("gcn2_rows", e0, t0)
                    if q == 6:
                        pe.wait_ge(flag(f"y_up{s}"), p + 1)
                        turned("gcn2_xt", e0, t2)
                    if q == 8:
                        pe.wait_ge(flag("gcn2_xt_read"), p + 1)
                        by_tiles("gcn2_mx", e0, t0, w["w2"])
                if s == HYPER:
                    if q == 2:
                        pe.wait_ge(acc_free, evictions(s, p))
                        turned("hyper_rows", e0, t0)
                        pe.wait_ge(flag("g_whole_up"), 1 + p + 1)
                        pe.wait_ge(flag("den_rows_up"), 1 + p + 1)
                        for k in range(KT):
                            mm(acc(p, k, 1), g_whole[:, k * P:(k + 1) * P], ones[:, 0:1], start=True, stop=False)
                            last = mm(acc(p, k, 1), t1[:, k * P:(k + 1) * P], pick[:, :], start=False, stop=True)
                        last.then_inc(flag("hyper_den"), 1)
                    if q == 6:
                        pe.wait_ge(flag("hyper_norm"), p + 1)
                if s == NORMED:
                    if q == 2:
                        pe.wait_ge(flag("normed_sx"), p + 1)
                        add_turned("normed_acc", p, t1)
                    if q == 6:
                        pe.wait_ge(acc_free, evictions(s, p))
                        by_tiles("normed_rows", e0, t0, w["w3"])

            def panel(s, p, done, dp):
                for q in range(PIECES):
                    finish(done, dp, q)
                    product(s, p, q)

            def read_sums(p):
                pe.wait_ge(flag("sums_steps"), PIECES * (p + 1))
                if p > 0:
                    pe.wait_ge(flag("d_bc_up"), p)
                sums_down("sums_read", E1, a_sum[:, p % 2, 0], a_sum[:, p % 2, 1])

            streamed_as = {n: m for m, (n, _, _) in enumerate(SMOOTHED)}
            for p in range(PANELS):
                for t in range(PIECES):
                    if p > 0:
                        finish(SUMS, p - 1, t - 4)
                    n = PIECES * p + t
                    if n in streamed_as:
                        product_early(streamed_as[n])
                    else:
                        pe.wait_ge(flag("sums_steps"), n + 1)
                        pe.wait_ge(raw_free, RAW + n)
                        pe.sem_inc(raw_free, 1)
                if p == 0:
                    pe.wait_ge(consts_in, 16 * 10)
                    pe.wait_ge(consts_up, 6)
                read_sums(p)
            for i, ends in enumerate(LATE_ENDS):
                for end in ends:
                    finish(*end)
                product_early(len(EARLY) + i)
            for q in range(PIECES):
                finish(SMOOTH, 0, q)

            pe.wait_ge(flag("h_up"), PANELS)
            pe.wait_ge(flag("z_low"), PANELS)
            pe.wait_ge(flag("sq_col_up"), PANELS)
            with pe.Fori(0, PANELS) as p:
                for k in range(KT):
                    pe.wait_ge(flag("staged"), 2 * (KT * p + k + 1))
                    for i in range(8):
                        if i % CH == 0:
                            pe.wait_ge(flag("scores_out"), 4 * (KT * p + k) + i // CH + 1)
                        dst = chunk(ps, i)
                        mm(dst, z_tile_h[k % 2][:, :], chunk(zh, i), start=True, stop=False)
                        mm(dst, z_tile_h[k % 2][:, :], chunk(zl, i), start=False, stop=False)
                        last = mm(dst, z_tile_l[k % 2][:, :], chunk(zh, i), start=False, stop=False)
                        if i == 7:
                            last.then_inc(flag("staging_free"), 1)
                        last = mm(dst, ones_r[:, :], chunk(h_rows, i), start=False, stop=True)
                        if i % CH == CH - 1:
                            last.then_inc(flag("scores_up"), 1)

            pe.wait_ge(flag("scores_out"), 4 + 4 * N // P)
            panel(KNN, 0, NEAR, 3)
            with pe.Fori(1, PANELS) as p:
                panel(KNN, p, KNN, p - 1)
            for s in range(GCN1, NORMED + 1):
                panel(s, 0, s - 1, 3)
                with pe.Fori(1, PANELS) as p:
                    panel(s, p, s, p - 1)
            for q in range(PIECES):
                finish(NORMED, 3, q)


def kernel(**inputs):
    import numpy as np
    import concourse.bacc as bacc
    from concourse.bass_utils import run_bass_kernel_spmd as run

    nc = bacc.Bacc("TRN2", target_bir_lowering=False, num_devices=1)
    at = np.ascontiguousarray(np.asarray(inputs["adj"]).T.reshape(PIECES, JT, P, PANELS, PW).transpose(3, 0, 2, 1, 4))
    x = np.ascontiguousarray(np.asarray(inputs["x"]).reshape(PANELS, KT, P, D).transpose(0, 2, 1, 3)
                             .reshape(PANELS, P, KT * D))
    arrays = {"at": at, "x_in": x}
    for short, name in (("w01", "L0_gnn_W1"), ("b01", "L0_gnn_b1"), ("w02", "L0_gnn_W2"), ("b02", "L0_gnn_b2"),
                        ("w11", "L1_gnn_W1"), ("b11", "L1_gnn_b1"), ("w12", "L1_gnn_W2"), ("b12", "L1_gnn_b2"),
                        ("w2", "L2_gnn_W"), ("w3", "L3_gnn_weight")):
        arrays[short] = np.ascontiguousarray(np.asarray(inputs[name]))
    args = [nc.dram_tensor(n, a.shape, mybir.dt.from_np(a.dtype), kind="ExternalInput").ap() for n, a in arrays.items()]
    out = nc.dram_tensor("out", [PANELS, P, KT * D], F32, kind="ExternalOutput").ap()
    build(nc, *args, out)
    r = run(nc, [arrays], core_ids=[0])
    got = np.asarray(r.results[0]["out"]).reshape(PANELS, P, KT, D).transpose(0, 2, 1, 3)
    return np.ascontiguousarray(got.reshape(N, D))
```

```python
import math

import numpy as np

import concourse.bass as bass
from concourse import mybir
from concourse.alu_op_type import AluOpType as ALU
from contextlib import ExitStack

F32 = mybir.dt.float32
F32R = mybir.dt.float32r
U32 = mybir.dt.uint32
ACT = mybir.ActivationFunctionType
AX = mybir.AxisListType

N, D, P = 4096, 128, 128
PANELS = 4
PW = N // PANELS
KT = PW // P
PIECES = 16
JT = N // P // PIECES
BANK = 512
CH = PW // BANK
RAW = 8
HI = 4
LN_EPS, L3_EPS, TOP = 1e-5, 1e-6, 4
CLIP, MIN_NORM, TINY = float(np.float32(1.0 - 1e-5)), 1e-15, 1e-10
ARTANH_CLIP = 0.5 * math.log((1.0 + CLIP) / (1.0 - CLIP))

SUMS, SMOOTH, KNN, GCN1, GCN2, HYPER, NORMED = range(7)
BUF = {SMOOTH: 0, KNN: 0, GCN1: 1, GCN2: 0, HYPER: 1, NORMED: 0}
ZBUF = 1
PER_X = PIECES // PANELS


def summed_piece(p, t):
    return (t + PER_X * (p + 1)) % PIECES


EARLY = [(p * PIECES + t, p, summed_piece(p, t)) for p in range(1, PANELS)
         for t in range(PIECES - PER_X * (p + 1), PIECES)]
LATE = [(2, q) for q in range(12, 16)] + [(1, q) for q in range(8, 16)] + [(0, q) for q in range(16)]
SUMMED = PANELS * PIECES
SMOOTHED = EARLY + [(SUMMED + i, p, q) for i, (p, q) in enumerate(LATE)]
STREAMED_AS = {n: m for m, (n, _, _) in enumerate(SMOOTHED)}
DONE_AT = {p: 1 + max(n for n, a, _ in SMOOTHED if a == p) for p in range(PANELS)}
assert sorted((p, q) for _, p, q in SMOOTHED) == [(p, q) for p in range(PANELS) for q in range(PIECES)]
assert len(EARLY) % HI == 0
LATE_ENDS = [[] for _ in LATE]
LATE_ENDS[0] = [(SUMS, 3, 4)]
for i, (p, step) in enumerate((p, step) for p in (3, 2, 1) for step in range(PIECES)):
    LATE_ENDS[1 + i // 2].append((SMOOTH, p, step))
POOL_FIRST = [n % 4 != 3 if n < SUMMED else n % 4 == 3 for n, _, _ in SMOOTHED]
POOL_Q = {KNN: (), GCN1: (3, 7, 11, 15), GCN2: (1, 3, 5, 9, 13),
          HYPER: (0, 2, 4, 6, 8, 10, 12, 14), NORMED: (1, 3, 5, 7, 9, 12, 15)}
POOL_Q_FIRST = {KNN: (0, 1)}


def is_first(p):
    return isinstance(p, int) and p == 0


def pool_q(s, p):
    return POOL_Q_FIRST.get(s, POOL_Q[s]) if is_first(p) else POOL_Q[s]


BACKWARD = (KNN, GCN2, NORMED)


def piece_at(s, t):
    return t if s in BACKWARD else (PANELS - 1 - t // PER_X) * PER_X + t % PER_X


def kept(s, p, t):
    return s > KNN and is_first(p) and t < PER_X


assert PER_X == HI
for r in range(GCN1, NORMED + 1):
    assert [piece_at(r, t) for t in range(PER_X)] == [piece_at(r - 1, PIECES - PER_X + t) for t in range(PER_X)]
G_PE = (4, 6, 7, 9, 11, 12, 13)
G_DVE = tuple(q for q in range(PIECES) if q not in G_PE)
G_PE_FIRST = (0, 1, 2, 3, 9, 12, 13)
G_DVE_FIRST = tuple(q for q in range(PIECES) if q not in G_PE_FIRST)


def g_pe(p):
    return G_PE_FIRST if is_first(p) else G_PE


def g_dve(p):
    return G_DVE_FIRST if is_first(p) else G_DVE


STREAMED = range(SMOOTH, NORMED + 1)
NEAR = -1


def build(nc, at, x, w01, b01, w02, b02, w11, b11, w12, b12, w2, w3, out):
    x_dram = {SUMS: x, NEAR: x, KNN: x, GCN2: nc.dram_tensor("x_after_0", [PANELS, P, KT * D], F32).ap(),
              HYPER: nc.dram_tensor("x_after_1", [PANELS, P, KT * D], F32).ap(),
              NORMED: nc.dram_tensor("x_after_2", [PANELS, P, KT * D], F32).ap()}
    scaled_rows = nc.dram_tensor("scaled_rows", [N, D], F32).ap()

    ctx = ExitStack()
    with ctx:
        def sem(name):
            return ctx.enter_context(nc.semaphore(name))

        arena_bytes = 211968
        ctx.enter_context(nc.sbuf_tensor("arena", [P, arena_bytes // 4], F32))
        base = nc.sbuf_base - arena_bytes
        top = [base]

        def at_byte(name, shape, dtype, offset):
            return nc.alloc_sbuf_tensor_at(name, [P, *shape], dtype, offset=offset)

        def place(name, shape, dtype):
            size = 4
            for s in shape:
                size *= s
            offset = top[0]
            top[0] += (size + 31) // 32 * 32
            assert top[0] <= base + arena_bytes, name
            return at_byte(name, shape, dtype, offset), offset

        raw, raw_at = place("raw", [RAW, JT, PW], F32)
        low = at_byte("low", [RAW, JT, PW], F32R, raw_at)
        high, high_at = place("high", [HI, JT, PW], F32R)
        scores = [at_byte(f"scores{i}", [N], F32, high_at + i * 4 * N) for i in range(2)]
        (xh0, _), (xh1, xh1_at) = [place(f"xh{i}", [N // P, D], F32R) for i in range(2)]
        xh = [xh0, xh1]
        a_sum = at_byte("a_sum", [2, JT, PW], F32, xh1_at)
        xl = [place(f"xl{i}", [N // P, D], F32R)[0] for i in range(2)]
        zh = xh[ZBUF][:, :, :].rearrange("p t d -> p (t d)")
        zl = xl[ZBUF][:, :, :].rearrange("p t d -> p (t d)")
        d_bc, d_at = place("d_bc", [N], F32)
        h_rows = at_byte("h_rows", [N], F32R, d_at)
        gathered = at_byte("gathered", [KT, TOP, D], F32, d_at)
        g_sum = at_byte("g_sum", [PW], F32, d_at)
        g_whole = at_byte("g_whole", [PW], F32, d_at + 4 * PW)
        t0, _ = place("t0", [PW], F32)
        t1, _ = place("t1", [PW], F32)
        t2, _ = place("t2", [PW], F32)
        xr, _ = place("xr", [PW], F32)
        w_names = ("w01", "w02", "w11", "w12", "w2", "w3")
        w = {n: place(n + "_sb", [D], F32)[0] for n in w_names}
        b02_bc, _ = place("b02_bc", [D], F32)
        b_cols, _ = place("b_cols", [3], F32)
        ident, _ = place("ident", [P], F32)
        ones, _ = place("ones", [P], F32)
        neg_half, _ = place("neg_half", [P], F32)
        ones_r, _ = place("ones_r", [P], F32R)
        z_tile_h = [place(f"z_tile_h{i}", [P], F32R)[0] for i in range(2)]
        z_tile_l = [place(f"z_tile_l{i}", [P], F32R)[0] for i in range(2)]
        top_v, _ = place("top_v", [KT, 8], F32)
        top_i, _ = place("top_i", [KT, 8], U32)
        near_i, _ = place("near_i", [N // P, TOP], U32)
        near_s, _ = place("near_s", [N // P, TOP], F32)
        ids, _ = place("ids", [TOP, KT], U32)
        dist, _ = place("dist", [KT, TOP], F32)
        a_rows, _ = place("a_rows", [N // P], F32)
        d_col, _ = place("d_col", [N // P], F32)
        s_col, _ = place("s_col", [N // P], F32)
        d2_col, _ = place("d2_col", [N // P], F32)
        sq_col, _ = place("sq_col", [N // P], F32)
        g_col, _ = place("g_col", [N // P], F32)
        g_parts, _ = place("g_parts", [2 * N // P + P], F32R)
        pick, _ = place("pick", [1], F32)
        stats, _ = place("stats", [KT, 6], F32)
        mv, _ = place("mv", [KT, 2], F32)
        c, _ = place("c", [16, KT], F32)

        ps = ctx.enter_context(nc.psum_tensor("ps", [P, 8 * BANK], F32))
        E0, E1 = 4 * BANK, 6 * BANK
        e0, e1 = ps[:, E0:E0 + PW], ps[:, E1:E1 + PW]

        def acc(p, lo=0, n=PW, s=None):
            if s == SMOOTH and p == 3:
                return ps[:, E0 + lo:E0 + lo + n]
            return ps[:, bass.ds(p % 2 * PW + lo, n)]

        def part(t, p, n=PW):
            return t[:, bass.ds(p * n, n)]

        def rows(t):
            return t.rearrange("p (t d) -> p t d", d=D)

        def tiles(t, p):
            return t[:, bass.ds(p * KT, KT), :]

        def place(s, p):
            return p * -1 + (PANELS - 1) if s in BACKWARD else p

        def g_place(p):
            return g_parts[:, bass.ds(p * (2 * KT), 2 * KT)].rearrange("p (k i) -> p k i", i=2)

        def bc(t, n=D):
            return t.unsqueeze(2).to_broadcast([P, KT, n])

        loaded = [sem(f"loaded{i}") for i in range(RAW)]
        raw_free = sem("raw_free")
        hi_ready, lo_dve, lo_pool = sem("hi_ready"), sem("lo_dve"), sem("lo_pool")
        acc_free = sem("acc_free")
        consts_in, consts_up = sem("consts_in"), sem("consts_up")
        xr_in, xr_used = sem("xr_in"), sem("xr_used")
        act_step = sem("act_step")
        S = {}

        def flag(name):
            if name not in S:
                S[name] = sem(name)
            return S[name]

        x_ready = {s: sem(f"x_ready{s}") for s in STREAMED}
        gathers = [sem(f"gathers{n}") for n in range(TOP)]
        g_used = sem("g_used")
        x_stored = {s: sem(f"x_stored{s}") for s in (KNN, GCN2, HYPER, NORMED)}
        rows_stored = sem("rows_stored")

        def wait_apart(eng, which, value):
            eng.wait_ge(which, value)
            eng.sem_inc(flag("waited"), 1)

        class Chain:

            def __init__(self, eng, name, per):
                self.eng, self.sem, self.per = eng, flag(name), per

            def begin(self, p):
                self.p, self.k = p, 0

            def link(self, *ins, apart=False):
                for i in ins:
                    self.k += 1
                    i.then_inc(self.sem, 1)
                if apart:
                    wait_apart(self.eng, self.sem, self.per * self.p + self.k)
                else:
                    self.eng.wait_ge(self.sem, self.per * self.p + self.k)

            def end(self):
                assert self.k == self.per, (self.k, self.per)

        def weighed(p, q):
            before = 0 if is_first(p) else p * len(G_DVE) + (len(G_DVE_FIRST) - len(G_DVE))
            return (before + sum(r <= q for r in g_dve(p))) * JT

        def piece(s, p, q):
            return 16 * (4 * (s - SMOOTH) + p) + q

        def consumed(s, p, q):
            return RAW + len(LATE) + piece(s, p, q) + 1

        def slot_of(s, q):
            return (SUMMED + len(LATE) + PER_X * (KNN - s) + q) % RAW

        def slot_use(s, p, q):
            before = SUMMED + len(LATE) + (PANELS * PIECES - PER_X) * (s - KNN)
            return (p * (PIECES // RAW) + ((before + q) // RAW + 1)) * 16

        def hi_count(s, p, q):
            return piece(s, p, q) + 1 - PER_X * (s - KNN)

        def low_count(s, p, q):
            mine = q in pool_q(s, p)

            def among(r, p, ts=range(PIECES)):
                return sum((t in pool_q(r, p)) == mine for t in ts if not kept(r, p, t))
            n = POOL_FIRST.count(mine) + sum(among(r, i) for r in range(KNN, s) for i in range(PANELS))
            if is_first(p):
                return mine, n + among(s, 0, range(q + 1))
            return mine, p * among(s, 1) + (n + among(s, 0) - among(s, 1) + among(s, 1, range(q + 1)))

        def evictions(s, p):
            return 2 + 4 * (s - SMOOTH) + p + 1

        def smooth_ended(p):
            return PANELS - p

        def ends_with(s, done, t):
            if done == NEAR:
                return range(4 * t, 4 * t + 4) if t < 4 else ()
            if s == done == KNN:
                return (t - 3,) if t >= 3 else ()
            if done == KNN:
                return {5: (0, 1), 6: (2, 3), 7: (4, 5), 8: (6, 7), 9: (8,), 10: (9,), 11: (10,)}.get(t, ())
            return (t,)

        XR_USERS = (SUMS, NEAR, KNN, GCN2, HYPER, NORMED)

        def xr_count(user, p):
            return 4 * XR_USERS.index(user) + p + 1

        block = ctx.enter_context(nc.Block())

        @block.sync
        def _(sp):
            sp.sem_inc(raw_free, RAW)
            in_turn = [(p, summed_piece(p, t)) for p in range(PANELS) for t in range(PIECES)] + LATE
            for n, (p, q) in enumerate(in_turn):
                sp.wait_ge(raw_free, n + 1)
                sp.dma_start(raw[:, n % RAW, :, :], at[p, q]).then_inc(loaded[n % RAW], 16)

            def stream(s, p, t):
                if not kept(s, p, t):
                    n, lies = p * PIECES + (consumed(s, 0, t) - RAW), place(s, p)
                    if not is_first(p):
                        n, lies = sp.snap(n), sp.snap(lies)
                    wait_apart(sp, raw_free, n)
                    sp.dma_start(raw[:, slot_of(s, t), :, :],
                                 at[bass.ds(lies, 1), piece_at(s, t)].rearrange("o p j i -> (o p) j i"))\
                      .then_inc(loaded[slot_of(s, t)], 16)

            for s in range(KNN, NORMED + 1):
                for t in range(PIECES):
                    stream(s, 0, t)
                with sp.Fori(1, PANELS) as p:
                    for t in range(PIECES):
                        stream(s, p, t)

        @block.gpsimd
        def _(pool):
            pool.memset(ident[:, :], 0.0).then_inc(consts_up, 1)
            pool.memset(ones[:, :], 1.0).then_inc(consts_up, 1)
            pool.memset(neg_half[:, :], -0.5).then_inc(consts_up, 1)
            pool.wait_ge(consts_up, 3)
            pool.affine_select(out=ident[:, :], in_=ident[:, :], compare_op=ALU.not_equal, fill=1.0,
                               base=0, pattern=[[-1, P]], channel_multiplier=1).then_inc(consts_up, 1)
            pool.tensor_copy(ones_r[:, :], ones[:, :]).then_inc(consts_up, 1)
            pool.sem_inc(flag("staging_free"), 2)
            pool.memset(g_parts[:, 2 * N // P:].bitcast(F32), 0.0).then_inc(flag("g_padded"), 1)
            pool.sem_inc(g_used, TOP)

            def low_part(s, p, q):
                slot = slot_of(s, q)
                pool.wait_ge(hi_ready, hi_count(s, p, q))
                if s == HYPER and q in g_dve(p):
                    pool.wait_ge(flag("g_sum_steps"), weighed(p, q))
                pool.tensor_tensor(low[:, slot], raw[:, slot], high[:, q % HI].bitcast(F32), ALU.subtract)\
                    .then_inc(lo_pool, 1)

            def finish(s, p, q):
                if s == NORMED and q == 1:
                    pool.wait_ge(xr_in, 16 * xr_count(NORMED, p))
                    pool.wait_ge(flag("normed_acc"), 1 + p)
                    pool.tensor_tensor(rows(t1[:, :]), rows(xr[:, :]), bc(part(s_col, place(s, p), KT)), ALU.mult)\
                        .then_inc(flag("normed_sx"), 1)

            def panel(s, p, done, dp):
                for q in range(PIECES):
                    if q in pool_q(s, p) and not kept(s, p, q):
                        low_part(s, p, q)
                    for step in ends_with(s, done, q):
                        finish(done, dp, step)

            for m, (n, _, _) in enumerate(SMOOTHED):
                if POOL_FIRST[m]:
                    pool.wait_ge(hi_ready, m + 1)
                    if n < SUMMED:
                        pool.wait_ge(flag("sums_steps"), n + 1)
                    pool.tensor_tensor(low[:, n % RAW], raw[:, n % RAW], high[:, m % HI].bitcast(F32), ALU.subtract)\
                        .then_inc(lo_pool, 1)

            pool.wait_ge(flag("z_low"), PANELS)
            with pool.Fori(0, PANELS) as p:
                for k in range(KT):
                    pool.wait_ge(flag("staging_free"), KT * p + k + 1)
                    for src, dst in ((zh, z_tile_h), (zl, z_tile_l)):
                        pool.tensor_copy(dst[k % 2][:, :], src[:, bass.ds(p * PW + k * P, P)].bitcast(F32))\
                            .then_inc(flag("staged"), 1)

            for t in range(PIECES):
                if t in pool_q(KNN, 0):
                    low_part(KNN, 0, t)

            pool.wait_ge(consts_in, 16 * 10)
            pool.wait_ge(rows_stored, 16 + 16 * PANELS)
            with pool.Fori(0, PANELS) as p:
                for n in range(TOP):
                    pool.wait_ge(g_used, TOP * p + n + 1)
                    pool.tensor_copy(ids[:, n, :], tiles(near_i, place(KNN, p))[:, :, n]).then_inc(flag("ids_up"), 1)
                    wait_apart(pool, flag("ids_up"), TOP * p + n + 1)
                    for k in range(KT):
                        pool.indirect_dma_start(
                            out=gathered[:, k, n, :], out_offset=None, in_=scaled_rows[:, :],
                            in_offset=bass.IndirectOffsetOnAxis(ap=ids[:, n, k:k + 1], axis=0),
                        ).then_inc(gathers[n], 16)
                pool.wait_ge(xr_in, 16 * xr_count(KNN, p))
                pool.tensor_tensor(rows(xr[:, :]), rows(xr[:, :]),
                                   b02_bc[:, :].unsqueeze(1).to_broadcast([P, KT, D]), ALU.add)\
                    .then_inc(flag("knn_xb"), 1)

            for s in range(GCN1, NORMED + 1):
                panel(s, 0, s - 1, 3)
                with pool.Fori(1, PANELS) as p:
                    panel(s, p, s, p - 1)
            for q in range(PIECES):
                finish(NORMED, 3, q)

        @block.scalar
        def _(act):
            for dst, src in ((w["w01"], w01), (w["w02"], w02), (w["w11"], w11), (w["w12"], w12), (w["w2"], w2),
                             (w["w3"], w3)):
                act.dma_start(dst[:, :], src).then_inc(consts_in, 16)
            act.dma_start(b02_bc[:, :], b02.partition_broadcast(P)).then_inc(consts_in, 16)
            for i, b in enumerate((b01, b11, b12)):
                act.dma_start(b_cols[:, i:i + 1], b.rearrange("(p o) -> p o", o=1)).then_inc(consts_in, 16)
            act.sem_inc(flag("scores_out"), 4)
            act.wait_ge(consts_in, 16 * 10)
            near_chain = Chain(act, "near_act", 1)

            def high_part(s, p, q):
                act.wait_ge(loaded[slot_of(s, q)], slot_use(s, p, q))
                if s == KNN and isinstance(p, int) and q < HI:
                    act.wait_ge(flag("searched"), 2 + N // P - (q < HI // 2))
                act.wait_ge(raw_free, consumed(s, p, q) - HI)
                act.activation(high[:, q % HI], raw[:, slot_of(s, q)], ACT.Copy).then_inc(hi_ready, 1)

            def high_early(m):
                n = SMOOTHED[m][0]
                act.wait_ge(loaded[n % RAW], 16 * (n // RAW + 1))
                if m >= HI:
                    act.wait_ge(raw_free, RAW + SMOOTHED[m - HI][0] + 1)
                act.activation(high[:, m % HI], raw[:, n % RAW], ACT.Copy).then_inc(hi_ready, 1)

            def load_x(user, p):
                act.wait_ge(xr_used, xr_count(user, p))
                if user in (GCN2, HYPER, NORMED):
                    act.wait_ge(x_stored[{GCN2: KNN, HYPER: GCN2, NORMED: HYPER}[user]], 16 + 16 * PANELS)
                act.dma_start(xr[:, :], x_dram[user][bass.ds(place(user, p), 1)].rearrange("o p n -> (o p) n")).then_inc(xr_in, 16)

            def store_x(s, p):
                act.wait_ge(flag(f"y_up{s}"), p + 1)
                dst = out if s == NORMED else x_dram[{KNN: GCN2, GCN2: HYPER, HYPER: NORMED}[s]]
                act.dma_start(dst[bass.ds(place(s, p), 1)].rearrange("o p n -> (o p) n"), t2[:, :]).then_inc(x_stored[s], 16)

            def read_acc(p, func=ACT.Copy, **kw):
                act.activation(t0[:, :], acc(p), func, **kw).then_inc(acc_free, 1)

            def finish(s, p, q):
                if q == 0 and s in XR_USERS:
                    load_x(s, p)

                if s == SUMS:
                    if q == 1:
                        act.wait_ge(flag("sums_shifted"), p + 1)
                        act.activation(c[:, 0:2, :], c[:, 0:2, :], ACT.Sqrt).then_inc(flag("sums_roots"), 1)
                    if q == 3:
                        act.wait_ge(flag("sums_dx"), p + 1)
                        act.activation(tiles(xh[0], place(s, p)), rows(t2[:, :]), ACT.Copy).then_inc(flag("sums_xh"), 1)
                    if q == 4:
                        act.wait_ge(flag("sums_d_bc"), p + 1)
                        act.activation(part(d_bc, place(s, p), PW), e1, ACT.Copy).then_inc(flag("d_bc_up"), 1)

                if s == SMOOTH:
                    if q == 5:
                        act.wait_ge(flag("smooth_w"), smooth_ended(p))
                        act.activation(t1[:, :], e0, ACT.Identity, bias=b_cols[:, 0:1]).then_inc(flag("smooth_b"), 1)
                    if q == 7:
                        act.wait_ge(flag("smooth_z"), smooth_ended(p))
                        act.activation(part(zh, place(s, p), PW), t1[:, :], ACT.Copy).then_inc(flag("z_high"), 1)
                        act.activation(t2[:, :], t1[:, :], ACT.Square).then_inc(flag("z_square"), 1)
                    if q == 10:
                        act.wait_ge(flag("z_norms"), smooth_ended(p))
                        act.activation(part(h_rows, place(s, p), PW), e1, ACT.Copy).then_inc(flag("h_high"), 1)
                        act.activation(part(sq_col, place(s, p), KT), ps[:, E0:E0 + KT], ACT.Copy).then_inc(flag("sq_col_up"), 1)

                if s == NEAR:
                    if q == 1:
                        near_chain.begin(p)
                        act.wait_ge(flag("near_d2"), p + 1)
                        near_chain.link(act.activation(dist[:, :, :], dist[:, :, :], ACT.Sqrt))
                        act.activation(tiles(near_s, place(s, p)), dist[:, :, :], ACT.Exp, scale=-0.5)\
                            .then_inc(flag("near_s_up"), 1)
                        near_chain.end()
                    if q == 4:
                        act.wait_ge(flag("near_sums"), p + 1)
                        act.activation(c[:, 0, :], c[:, 0, :], ACT.Sqrt).then_inc(flag("near_roots"), 1)
                    if q == 7:
                        act.wait_ge(flag("near_dx"), p + 1)
                        act.activation(tiles(xh[0], place(s, p)), rows(t0[:, :]), ACT.Copy).then_inc(flag("near_xh"), 1)
                        act.dma_start(scaled_rows[bass.ds(p * PW, PW), :].rearrange("(t p) d -> p t d", p=P),
                                      rows(t0[:, :])).then_inc(rows_stored, 16)

                if s == KNN:
                    if q == 5:
                        act.wait_ge(flag("knn_acc"), p + 1)
                        read_acc(p)
                    if q == 9:
                        root(s, p)
                    if q == 10:
                        rounded_x(s, p)
                        store_x(s, p)

                if s == GCN1:
                    if q == 1:
                        act.wait_ge(raw_free, consumed(s, p, PIECES - 1))
                        read_acc(p)
                    if q == 5:
                        act.wait_ge(flag("gcn1_w"), p + 1)
                        act.activation(t1[:, :], e0, ACT.Relu, bias=b_cols[:, 1:2]).then_inc(flag("gcn1_h"), 1)
                    if q == 9:
                        act.wait_ge(flag("gcn1_rows"), p + 1)
                        act.activation(tiles(xh[BUF[GCN2]], place(s, p)), rows(e1), ACT.Copy).then_inc(flag("gcn1_xh"), 1)

                if s == GCN2:
                    if q == 1:
                        act.wait_ge(raw_free, consumed(s, p, PIECES - 1))
                        read_acc(p, ACT.Relu, bias=b_cols[:, 2:3])
                    if q == 5:
                        root(s, p)
                    if q == 6:
                        act.wait_ge(flag(f"y_up{s}"), p + 1)
                        store_x(s, p)
                        act.activation(t1[:, :], t2[:, :], ACT.Square).then_inc(flag("gcn2_x_sq"), 1)
                    if q == 7:
                        act.wait_ge(flag("gcn2_x_norm"), p + 1)
                        act.activation(c[:, 2, :], c[:, 0, :], ACT.Sqrt).then_inc(flag("gcn2_x_root"), 1)
                    if q == 8:
                        act.wait_ge(flag("gcn2_xt"), p + 1)
                        act.activation(t0[:, :], e0, ACT.Copy).then_inc(flag("gcn2_xt_read"), 1)
                        act.wait_ge(flag("gcn2_ratio"), p + 1)
                        act.activation(c[:, 5, :], c[:, 5, :], ACT.Ln).then_inc(flag("gcn2_ln"), 1)
                    if q == 10:
                        act.wait_ge(flag("gcn2_mx"), p + 1)
                        act.activation(t1[:, :], e0, ACT.Square).then_inc(flag("gcn2_mx_sq"), 1)
                    if q == 11:
                        act.wait_ge(flag("gcn2_mx_norm"), p + 1)
                        act.activation(c[:, 3, :], c[:, 1, :], ACT.Sqrt).then_inc(flag("gcn2_mx_root"), 1)
                    if q == 12:
                        act.wait_ge(flag("gcn2_arg"), p + 1)
                        act.activation(c[:, 5, :], c[:, 5, :], ACT.Tanh).then_inc(flag("gcn2_tanh"), 1)
                    if q == 13:
                        g_high = g_place(place(s, p))[:, :, 0]
                        act.wait_ge(flag("gcn2_g"), p + 1)
                        act.activation(g_high, part(g_col, place(s, p), KT), ACT.Copy)\
                           .then_inc(flag("gcn2_g_high"), 1)
                        rounded_x(s, p)

                if s == HYPER:
                    if q == 1:
                        act.wait_ge(raw_free, consumed(s, p, PIECES - 1))
                        read_acc(p)
                        act.activation(t1[:, :], e1, ACT.Copy).then_inc(flag("den_rows_up"), 1)
                    if q == 4:
                        act.wait_ge(flag("hyper_den"), 1 + p + 1)
                        act.activation(t1[:, :], e0, ACT.Square).then_inc(flag("hyper_sq"), 1)
                    if q == 5:
                        act.wait_ge(flag("hyper_norm"), p + 1)
                        act.activation(c[:, 0, :], c[:, 0, :], ACT.Sqrt).then_inc(flag("hyper_root"), 1)
                    if q == 6:
                        act.wait_ge(flag("hyper_ratio"), p + 1)
                        act.activation(c[:, 5, :], c[:, 5, :], ACT.Ln).then_inc(flag("hyper_ln"), 1)
                    if q == 7:
                        act.wait_ge(flag("hyper_u"), p + 1)
                        act.activation(t0[:, :], t1[:, :], ACT.Square).then_inc(flag("hyper_u_sq"), 1)
                    if q == 8:
                        act.wait_ge(flag("hyper_u_norm"), p + 1)
                        act.activation(c[:, 0, :], c[:, 0, :], ACT.Sqrt).then_inc(flag("hyper_u_root"), 1)
                    if q == 9:
                        act.wait_ge(flag("hyper_un"), p + 1)
                        act.activation(c[:, 1, :], c[:, 0, :], ACT.Tanh).then_inc(flag("hyper_u_tanh"), 1)
                    if q == 10:
                        root(s, p)
                    if q == 11:
                        store_x(s, p)
                        rounded_x(s, p)

                if s == NORMED:
                    if q == 4:
                        act.wait_ge(flag("normed_acc"), 1 + p + 1)
                        read_acc(p)
                    if q == 8:
                        root(s, p)
                    if q == 9:
                        store_x(s, p)

            def root(s, p):
                act.wait_ge(flag(f"var_up{s}"), p + 1)
                act.activation(c[:, 14, :], c[:, 14, :], ACT.Sqrt).then_inc(flag(f"root_up{s}"), 1)

            def rounded_x(s, p):
                src = {KNN: t2, GCN2: t1, HYPER: t0}[s]
                act.wait_ge(flag(f"new_x{s}"), p + 1)
                act.activation(tiles(xh[BUF[s + 1]], place(s, p)), rows(src[:, :]), ACT.Copy).then_inc(flag(f"new_xh{s}"), 1)

            def panel(s, p, done, dp):
                for q in range(PIECES):
                    if not kept(s, p, q):
                        high_part(s, p, q)
                    for step in ends_with(s, done, q):
                        finish(done, dp, step)

            for p in range(PANELS):
                for t in range(PIECES):
                    if p > 0 and t == 4:
                        finish(SUMS, p - 1, 4)
                    if t == 5:
                        finish(SUMS, p, 0)
                    if PIECES * p + t in STREAMED_AS:
                        high_early(STREAMED_AS[PIECES * p + t])
                finish(SUMS, p, 1)
                finish(SUMS, p, 3)
            for i, ends in enumerate(LATE_ENDS):
                high_early(len(EARLY) + i)
                for end in ends:
                    finish(*end)
            for q in range(PIECES):
                finish(SMOOTH, 0, q)

            def scores_out(p, q):
                k = q // 2
                if q % 2 == 0:
                    act.wait_ge(flag("searched"), KT * p + k + 1)
                for r in range(2):
                    pair = q % 2 * 2 + r
                    act.wait_ge(flag("scores_up"), 4 * (KT * p + k) + pair + 1)
                    act.activation(scores[k % 2][:, pair * PW:(pair + 1) * PW], ps[:, pair * PW:(pair + 1) * PW],
                                   ACT.Copy).then_inc(flag("scores_out"), 1)

            for q in range(PIECES):
                scores_out(0, q)
            with act.Fori(1, PANELS) as p:
                for q in range(PIECES):
                    scores_out(p, q)
                    finish(NEAR, p - 1, q)

            panel(KNN, 0, NEAR, 3)
            with act.Fori(1, PANELS) as p:
                panel(KNN, p, KNN, p - 1)
            for s in range(GCN1, NORMED + 1):
                panel(s, 0, s - 1, 3)
                with act.Fori(1, PANELS) as p:
                    panel(s, p, s, p - 1)
            for q in range(PIECES):
                finish(NORMED, 3, q)
            act.wait_ge(x_stored[NORMED], 16 + 16 * PANELS)

        @block.vector
        def _(dve):
            TT, TS, STT = dve.tensor_tensor, dve.tensor_scalar, dve.scalar_tensor_tensor
            near = Chain(dve, "near_dve", 3)
            picks = Chain(dve, "picks_dve", TOP * KT)
            ln = {s: Chain(dve, f"norm_dve{s}", n) for s, n in
                  ((KNN, 2 + 2 * KT + 1), (GCN2, 2 * KT + 1), (HYPER, 2 * KT + 1), (NORMED, 2 + 2 * KT + 1))}
            mob = Chain(dve, "mobius_dve", 17)
            hyp = Chain(dve, "hyper_dve", 23)
            dve.sem_inc(flag("searched"), 2)
            dve.sem_inc(acc_free, 2)
            for which in (xr_used, *(flag(n) for n in ("normed_acc", "g_whole_up", "hyper_den", "den_rows_up", "sums_read"))):
                dve.sem_inc(which, 1)
            for which in (rows_stored, *x_stored.values()):
                dve.sem_inc(which, 16)
            dve.wait_ge(consts_up, 5)
            TT(pick[:, :], ident[:, 0:1], ident[:, 1:2], ALU.add).then_inc(consts_up, 1)

            def add_piece(p, q):
                n = PIECES * p + q
                dve.wait_ge(loaded[n % RAW], 16 * (n // RAW + 1))
                if q == 0:
                    if p > 1:
                        dve.wait_ge(flag("sums_read"), p)
                    ins = dve.tensor_copy(a_sum[:, p % 2], raw[:, 0])
                else:
                    dve.wait_ge(flag("sums_steps"), n)
                    ins = TT(a_sum[:, p % 2], a_sum[:, p % 2], raw[:, q % RAW], ALU.add)
                ins.then_inc(flag("sums_steps"), 1)

            def low_early(m):
                n = SMOOTHED[m][0]
                dve.wait_ge(hi_ready, m + 1)
                if n < SUMMED:
                    dve.wait_ge(flag("sums_steps"), n + 1)
                TT(low[:, n % RAW], raw[:, n % RAW], high[:, m % HI].bitcast(F32), ALU.subtract).then_inc(lo_dve, 1)

            def low_part(s, p, q):
                slot = slot_of(s, q)
                dve.wait_ge(hi_ready, hi_count(s, p, q))
                if s == HYPER and q in g_dve(p):
                    dve.wait_ge(flag("g_sum_steps"), weighed(p, q))
                TT(low[:, slot], raw[:, slot], high[:, q % HI].bitcast(F32), ALU.subtract).then_inc(lo_dve, 1)

            def weigh_piece(p, q):
                dve.wait_ge(hi_ready, hi_count(HYPER, p, q))
                for j in range(JT):
                    n = JT * piece_at(HYPER, q) + j
                    src = raw[:, slot_of(HYPER, q), j]
                    if (q, j) == (g_dve(p)[0], 0):
                        dve.wait_ge(flag("g_whole_up"), 1 + p)
                        ins = TS(g_sum[:, :], src, g_col[:, n:n + 1], None, ALU.mult)
                    else:
                        dve.wait_ge(flag("g_sum_steps"), weighed(p, q) + (j - JT))
                        ins = STT(g_sum[:, :], src, g_col[:, n:n + 1], g_sum[:, :], ALU.mult, ALU.add)
                    ins.then_inc(flag("g_sum_steps"), 1)
                if q == g_dve(p)[-1]:
                    dve.wait_ge(flag("g_sum_steps"), weighed(p, q))
                    dve.wait_ge(flag("hyper_den"), 1 + p)
                    dve.tensor_copy(g_whole[:, :], g_sum[:, :]).then_inc(flag("g_whole_up"), 1)

            def variances(s, p, src):
                ch = ln[s]
                ch.link(*[dve.bn_stats(stats[:, k, :], rows(src[:, :])[:, k, :]) for k in range(KT)], apart=True)
                ch.link(*[dve.bn_aggr(mv[:, k, :], stats[:, k, :]) for k in range(KT)])
                TS(c[:, 14, :], mv[:, :, 1], LN_EPS, None, ALU.add).then_inc(flag(f"var_up{s}"), 1)

            def normalise(s, p, src):
                ch = ln[s]
                dve.wait_ge(flag(f"root_up{s}"), p + 1)
                ch.link(dve.reciprocal(c[:, 15, :], c[:, 14, :]))
                ch.end()
                dve.wait_ge(x_stored[s], 16 + 16 * p)
                if s == KNN:
                    dve.wait_ge(flag("knn_acc"), p + 1)
                for k in range(KT):
                    last = TS(rows(t2[:, :])[:, k, :], rows(src[:, :])[:, k, :], mv[:, k, 0:1], c[:, 15, k:k + 1],
                              ALU.subtract, ALU.mult)
                    if k < KT - 1:
                        last.then_inc(flag(f"y_part{s}"), 1)
                dve.wait_ge(flag(f"y_part{s}"), (KT - 1) * (p + 1))
                last.then_inc(flag(f"y_up{s}"), 1)

            def rest_of_x(s, p, src):
                dve.wait_ge(flag(f"new_xh{s}"), p + 1)
                TT(tiles(xl[BUF[s + 1]], place(s, p)), rows(src[:, :]), tiles(xh[BUF[s + 1]], place(s, p)).bitcast(F32), ALU.subtract)\
                    .then_inc(x_ready[s + 1], 1)
                dve.wait_ge(x_ready[s + 1], p + 1)

            def ratio(chain, src, lo, hi):
                chain.link(TS(c[:, lo, :], c[:, src, :], CLIP, None, ALU.min))
                chain.link(TS(c[:, hi, :], c[:, lo, :], 1.0, None, ALU.add),
                           TS(c[:, lo + 1, :], c[:, lo, :], -1.0, 1.0, ALU.mult, ALU.add))
                chain.link(dve.reciprocal(c[:, lo + 1, :], c[:, lo + 1, :]))
                return TT(c[:, hi, :], c[:, hi, :], c[:, lo + 1, :], ALU.mult)

            def finish(s, p, q):
                if s == SUMS:
                    if q == 0:
                        dve.wait_ge(flag("sums_read"), 1 + p + 1)
                        dve.tensor_copy(part(a_rows, place(s, p), KT), ps[:, E1:E1 + KT]).then_inc(flag("a_rows_up"), 1)
                        dve.tensor_copy(c[:, 0, :], ps[:, E1:E1 + KT]).then_inc(flag("a_rows_up"), 1)
                        TS(c[:, 1, :], ps[:, E1:E1 + KT], L3_EPS, None, ALU.add).then_inc(flag("sums_shifted"), 1)
                    if q == 2:
                        dve.wait_ge(flag("sums_roots"), p + 1)
                        dve.reciprocal(part(s_col, place(s, p), KT), c[:, 1, :]).then_inc(flag("s_col_up"), 1)
                        dve.reciprocal(part(d_col, place(s, p), KT), c[:, 0, :]).then_inc(flag("d_col_up"), 1)
                        dve.wait_ge(flag("d_col_up"), p + 1)
                        dve.wait_ge(xr_in, 16 * xr_count(SUMS, p))
                        TT(rows(t2[:, :]), rows(xr[:, :]), bc(part(d_col, place(s, p), KT)), ALU.mult).then_inc(flag("sums_dx"), 1)
                    if q == 3:
                        dve.wait_ge(flag("sums_xh"), p + 1)
                        TT(tiles(xl[0], place(s, p)), rows(t2[:, :]), tiles(xh[0], place(s, p)).bitcast(F32), ALU.subtract)\
                            .then_inc(x_ready[SMOOTH], 1)
                        dve.wait_ge(x_ready[SMOOTH], p + 1)
                        TT(rows(xr[:, :]), ident[:, :].unsqueeze(1).to_broadcast([P, KT, P]),
                           bc(part(d_col, place(s, p), KT), P), ALU.mult).then_inc(flag("sums_diag"), 1)

                if s == SMOOTH:
                    if q == 1:
                        dve.wait_ge(raw_free, RAW + DONE_AT[p])
                        dve.wait_ge(flag("d_bc_up"), PANELS)
                        TT(t0[:, :], acc(p, s=SMOOTH), part(d_bc, place(s, p), PW), ALU.mult).then_inc(acc_free, 1)
                    if q == 6:
                        dve.wait_ge(flag("smooth_b"), smooth_ended(p))
                        STT(t1[:, :], t1[:, :], 0.1, t1[:, :], ALU.mult, ALU.max).then_inc(flag("smooth_z"), 1)
                    if q == 8:
                        dve.wait_ge(flag("z_high"), smooth_ended(p))
                        TT(part(zl, place(s, p), PW), t1[:, :], part(zh, place(s, p), PW).bitcast(F32), ALU.subtract)\
                            .then_inc(flag("z_low"), 1)
                    if q == 11:
                        dve.wait_ge(flag("h_high"), smooth_ended(p))
                        h = part(h_rows, place(s, p), PW)
                        TT(t2[:, :], e1, h.bitcast(F32), ALU.subtract).then_inc(flag("h_low"), 1)
                        dve.wait_ge(flag("h_low"), 2 * smooth_ended(p) - 1)
                        TS(t2[:, :], t2[:, :], ident[:, 1:2], None, ALU.mult).then_inc(flag("h_low"), 1)
                        dve.wait_ge(flag("h_low"), 2 * smooth_ended(p))
                        STT(h, h.bitcast(F32), ident[:, 0:1], t2[:, :], ALU.mult, ALU.add).then_inc(flag("h_up"), 1)

                if s == NEAR:
                    if q == 0:
                        near.begin(p)
                        dve.wait_ge(flag("sq_col_up"), PANELS)
                        near.link(STT(dist[:, :, :], top_v[:, :, 0:TOP], -2.0, bc(part(sq_col, place(s, p), KT), TOP),
                                      ALU.mult, ALU.add))
                        TS(dist[:, :, :], dist[:, :, :], 0.0, TINY, ALU.max, ALU.add).then_inc(flag("near_d2"), 1)
                        near.link(dve.tensor_copy(tiles(near_i, place(s, p)), top_i[:, :, 0:TOP]))
                    if q == 3:
                        dve.wait_ge(flag("near_s_up"), p + 1)
                        near.link(dve.tensor_reduce(out=c[:, 1, :], in_=tiles(near_s, place(s, p)), op=ALU.add, axis=AX.X))
                        near.end()
                        TT(c[:, 0, :], c[:, 1, :], part(a_rows, place(s, p), KT), ALU.add).then_inc(flag("near_sums"), 1)
                    if q == 6:
                        dve.wait_ge(flag("near_roots"), p + 1)
                        dve.reciprocal(part(d2_col, place(s, p), KT), c[:, 0, :]).then_inc(flag("d2_col_up"), 1)
                        dve.wait_ge(flag("d2_col_up"), p + 1)
                        dve.wait_ge(xr_in, 16 * xr_count(NEAR, p))
                        dve.wait_ge(rows_stored, 16 + 16 * p)
                        TT(rows(t0[:, :]), rows(xr[:, :]), bc(part(d2_col, place(s, p), KT)), ALU.mult)\
                            .then_inc(flag("near_dx"), 1)
                    if q == 8:
                        dve.wait_ge(flag("near_xh"), p + 1)
                        TT(tiles(xl[0], place(s, p)), rows(t0[:, :]), tiles(xh[0], place(s, p)).bitcast(F32), ALU.subtract)\
                            .then_inc(x_ready[KNN], 1)
                        dve.wait_ge(x_ready[KNN], p + 1)
                        dve.sem_inc(xr_used, 1)

                if s == KNN:
                    if q == 0:
                        picks.begin(p)
                    if q < TOP:
                        dve.wait_ge(gathers[q], 16 * KT * (p + 1))
                        if q == 0:
                            dve.wait_ge(x_stored[KNN], 16 + 16 * p)
                        weighed_rows = []
                        for k in range(KT):
                            y = rows(t2[:, :])[:, k, :]
                            weight = near_s[:, bass.ds(place(s, p) * KT + k, 1), q:q + 1].rearrange("p o k -> p (o k)")
                            if q == 0:
                                ins = TS(y, gathered[:, k, 0, :], weight, None, ALU.mult)
                            else:
                                ins = STT(y, gathered[:, k, q, :], weight, y, ALU.mult, ALU.add)
                            weighed_rows.append(ins)
                        picks.link(*weighed_rows)
                        dve.sem_inc(g_used, 1)
                        if q == TOP - 1:
                            picks.end()
                            dve.sem_inc(flag("picked"), 1)
                    if q == 8:
                        dve.wait_ge(flag("knn_rows"), p + 1)
                        dve.wait_ge(flag("knn_xb"), p + 1)
                        ch = ln[s]
                        ch.begin(p)
                        ch.link(TT(rows(t1[:, :]), rows(e0), bc(part(d2_col, place(s, p), KT)), ALU.mult))
                        ch.link(TT(t1[:, :], t1[:, :], xr[:, :], ALU.add))
                        dve.sem_inc(xr_used, 1)
                        variances(s, p, t1)
                    if q == 9:
                        normalise(s, p, t1)
                        dve.wait_ge(flag(f"y_up{s}"), p + 1)
                        dve.sem_inc(flag(f"new_x{s}"), 1)
                    if q == 10:
                        rest_of_x(s, p, t2)

                if s == GCN1:
                    if q == 10:
                        dve.wait_ge(flag("gcn1_xh"), p + 1)
                        TT(tiles(xl[BUF[GCN2]], place(s, p)), rows(e1), tiles(xh[BUF[GCN2]], place(s, p)).bitcast(F32), ALU.subtract)\
                            .then_inc(x_ready[GCN2], 1)

                if s == GCN2:
                    if q == 4:
                        dve.wait_ge(flag("gcn2_rows"), p + 1)
                        dve.wait_ge(xr_in, 16 * xr_count(s, p))
                        ln[s].begin(p)
                        TT(t1[:, :], e0, xr[:, :], ALU.add).then_inc(xr_used, 1)
                        dve.wait_ge(xr_used, 1 + xr_count(s, p))
                        variances(s, p, t1)
                    if q == 5:
                        normalise(s, p, t1)
                    if q == 6:
                        dve.wait_ge(flag("gcn2_x_sq"), p + 1)
                        dve.tensor_reduce(out=c[:, 0, :], in_=rows(t1[:, :]), op=ALU.add, axis=AX.X)\
                           .then_inc(flag("gcn2_x_norm"), 1)
                    if q == 7:
                        mob.begin(p)
                        dve.wait_ge(flag("gcn2_x_root"), p + 1)
                        mob.link(TS(c[:, 2, :], c[:, 2, :], MIN_NORM, None, ALU.max))
                        ratio(mob, 2, 8, 5).then_inc(flag("gcn2_ratio"), 1)
                        mob.link(dve.reciprocal(c[:, 6, :], c[:, 2, :]))
                    if q == 8:
                        dve.wait_ge(flag("gcn2_ln"), p + 1)
                        mob.link(STT(c[:, 6, :], c[:, 5, :], 0.5, c[:, 6, :], ALU.mult, ALU.mult))
                    if q == 10:
                        dve.wait_ge(flag("gcn2_mx_sq"), p + 1)
                        dve.tensor_reduce(out=c[:, 1, :], in_=rows(t1[:, :]), op=ALU.add, axis=AX.X)\
                           .then_inc(flag("gcn2_mx_norm"), 1)
                    if q == 11:
                        dve.wait_ge(flag("gcn2_mx_root"), p + 1)
                        mob.link(TS(c[:, 3, :], c[:, 3, :], MIN_NORM, None, ALU.max))
                        TT(c[:, 5, :], c[:, 3, :], c[:, 6, :], ALU.mult).then_inc(flag("gcn2_arg"), 1)
                        mob.link(dve.reciprocal(c[:, 7, :], c[:, 3, :]))
                    if q == 12:
                        dve.wait_ge(flag("gcn2_tanh"), p + 1)
                        mob.link(TT(c[:, 5, :], c[:, 5, :], c[:, 7, :], ALU.mult))
                        mob.link(TT(c[:, 10, :], c[:, 1, :], c[:, 5, :], ALU.mult))
                        mob.link(TT(c[:, 10, :], c[:, 10, :], c[:, 5, :], ALU.mult))
                        mob.link(TS(c[:, 10, :], c[:, 10, :], -1.0, 1.0, ALU.mult, ALU.add))
                        mob.link(TS(c[:, 10, :], c[:, 10, :], 1e-5, None, ALU.max))
                        mob.link(dve.reciprocal(c[:, 10, :], c[:, 10, :]))
                        mob.link(TS(c[:, 10, :], c[:, 10, :], 2.0, None, ALU.mult))
                        TS(part(g_col, place(s, p), KT), c[:, 10, :], -1.0, None, ALU.add).then_inc(flag("gcn2_g"), 1)
                        mob.link(TT(c[:, 10, :], c[:, 10, :], c[:, 5, :], ALU.mult))
                        mob.end()
                        TT(rows(t1[:, :]), rows(e0), bc(c[:, 10, :]), ALU.mult).then_inc(flag(f"new_x{s}"), 1)
                    if q == 13:
                        g_pair = g_place(place(s, p))
                        g_high, g_low = g_pair[:, :, 0], g_pair[:, :, 1]
                        dve.wait_ge(flag("gcn2_g_high"), p + 1)
                        TT(g_low, part(g_col, place(s, p), KT), g_high.bitcast(F32), ALU.subtract).then_inc(flag("gcn2_g_low"), 1)
                        dve.wait_ge(flag("gcn2_g_low"), p + 1)
                        rest_of_x(s, p, t1)

                if s == HYPER:
                    if q == 4:
                        hyp.begin(p)
                        den = acc(p, 0, KT)
                        dve.wait_ge(flag("hyper_den"), 1 + p + 1)
                        hyp.link(TS(c[:, 2, :], den, TINY, None, ALU.max), TS(c[:, 3, :], den, -TINY, None, ALU.min),
                                 TS(c[:, 4, :], den, 0.0, None, ALU.is_ge))
                        hyp.link(TT(c[:, 2, :], c[:, 2, :], c[:, 3, :], ALU.subtract))
                        hyp.link(TT(c[:, 2, :], c[:, 2, :], c[:, 4, :], ALU.mult))
                        hyp.link(TT(c[:, 2, :], c[:, 2, :], c[:, 3, :], ALU.add))
                        hyp.link(dve.reciprocal(c[:, 2, :], c[:, 2, :]))
                        dve.wait_ge(flag("hyper_sq"), p + 1)
                        dve.tensor_reduce(out=c[:, 0, :], in_=rows(t1[:, :]), op=ALU.add, axis=AX.X)\
                           .then_inc(flag("hyper_norm"), 1)
                    if q == 5:
                        dve.wait_ge(flag("hyper_root"), p + 1)
                        hyp.link(TT(c[:, 1, :], c[:, 0, :], c[:, 2, :], ALU.mult))
                        hyp.link(STT(c[:, 1, :], c[:, 1, :], -1.0, c[:, 1, :], ALU.mult, ALU.max))
                        hyp.link(TS(c[:, 1, :], c[:, 1, :], MIN_NORM, None, ALU.max))
                        ratio(hyp, 1, 8, 5).then_inc(flag("hyper_ratio"), 1)
                        hyp.link(dve.reciprocal(c[:, 7, :], c[:, 1, :]))
                        hyp.link(TT(c[:, 2, :], c[:, 2, :], c[:, 7, :], ALU.mult))
                    if q == 6:
                        dve.wait_ge(flag("hyper_ln"), p + 1)
                        hyp.link(STT(c[:, 5, :], c[:, 5, :], 0.25, part(a_rows, place(s, p), KT), ALU.mult, ALU.mult))
                        hyp.link(TS(c[:, 5, :], c[:, 5, :], ARTANH_CLIP, -ARTANH_CLIP, ALU.min, ALU.max))
                        hyp.link(TT(c[:, 2, :], c[:, 2, :], c[:, 5, :], ALU.mult))
                        hyp.link(TT(rows(t1[:, :]), rows(e0), bc(c[:, 2, :]), ALU.mult))
                        TS(t1[:, :], t1[:, :], 0.0, None, ALU.max).then_inc(flag("hyper_u"), 1)
                    if q == 7:
                        dve.wait_ge(flag("hyper_u_sq"), p + 1)
                        dve.tensor_reduce(out=c[:, 0, :], in_=rows(t0[:, :]), op=ALU.add, axis=AX.X)\
                           .then_inc(flag("hyper_u_norm"), 1)
                    if q == 8:
                        dve.wait_ge(flag("hyper_u_root"), p + 1)
                        TS(c[:, 0, :], c[:, 0, :], MIN_NORM, None, ALU.max).then_inc(flag("hyper_un"), 1)
                        dve.wait_ge(flag("hyper_un"), p + 1)
                        hyp.link(dve.reciprocal(c[:, 3, :], c[:, 0, :]))
                    if q == 9:
                        dve.wait_ge(flag("hyper_u_tanh"), p + 1)
                        hyp.link(TT(c[:, 3, :], c[:, 3, :], c[:, 1, :], ALU.mult))
                        hyp.link(TT(rows(t1[:, :]), rows(t1[:, :]), bc(c[:, 3, :]), ALU.mult))
                        hyp.end()
                        dve.wait_ge(xr_in, 16 * xr_count(s, p))
                        TT(t1[:, :], t1[:, :], xr[:, :], ALU.add).then_inc(xr_used, 1)
                        dve.wait_ge(xr_used, 1 + xr_count(s, p))
                        ln[s].begin(p)
                        variances(s, p, t1)
                    if q == 10:
                        normalise(s, p, t1)
                        dve.wait_ge(flag(f"y_up{s}"), p + 1)
                        TT(rows(t0[:, :]), rows(t2[:, :]), bc(part(s_col, place(s, p), KT)), ALU.mult)\
                            .then_inc(flag(f"new_x{s}"), 1)
                    if q == 11:
                        rest_of_x(s, p, t0)

                if s == NORMED:
                    if q == 7:
                        dve.wait_ge(flag("normed_rows"), p + 1)
                        ch = ln[s]
                        ch.begin(p)
                        ch.link(TT(rows(t1[:, :]), rows(e0), bc(part(s_col, place(s, p), KT)), ALU.mult))
                        ch.link(TT(t1[:, :], t1[:, :], xr[:, :], ALU.add))
                        dve.sem_inc(xr_used, 1)
                        variances(s, p, t1)
                    if q == 8:
                        normalise(s, p, t1)

            def panel(s, p, done, dp):
                for q in range(PIECES):
                    if s == HYPER and q in g_dve(p):
                        weigh_piece(p, q)
                    if q not in pool_q(s, p) and not kept(s, p, q):
                        low_part(s, p, q)
                    for step in ends_with(s, done, q):
                        finish(done, dp, step)

            for p in range(PANELS):
                for t in range(PIECES):
                    add_piece(p, t)
                    if p > 0 and t == 0:
                        finish(SUMS, p - 1, 3)
                    own = [PIECES * p + t] if t < PIECES - PER_X else []
                    if t == PIECES - 1:
                        own = range(PIECES * (p + 1) - PER_X, PIECES * (p + 1))
                    for n in own:
                        if n in STREAMED_AS and not POOL_FIRST[STREAMED_AS[n]]:
                            low_early(STREAMED_AS[n])
                finish(SUMS, p, 0)
                finish(SUMS, p, 2)
            finish(SUMS, 3, 3)
            for i, ends in enumerate(LATE_ENDS):
                if not POOL_FIRST[len(EARLY) + i]:
                    low_early(len(EARLY) + i)
                for end in ends:
                    finish(*end)
            for q in range(PIECES):
                finish(SMOOTH, 0, q)

            def search(p, k):
                wait_apart(dve, flag("scores_out"), 4 + 4 * (KT * p + k + 1))
                dve.max(out=top_v[:, k, :], in_=scores[k % 2][:, :]).then_inc(flag("maxima"), 1)
                wait_apart(dve, flag("maxima"), KT * p + k + 1)
                dve.max_index(out=top_i[:, k, :], in_max=top_v[:, k, :], in_values=scores[k % 2][:, :])\
                   .then_inc(flag("searched"), 1)

            for k in range(KT):
                search(0, k)
            with dve.Fori(1, PANELS) as p:
                dve.wait_ge(flag("searched"), 2 + KT * p)
                finish(NEAR, p - 1, 0)
                for k in range(KT):
                    search(p, k)
                    for q in (2 * k + 1, 2 * k + 2):
                        finish(NEAR, p - 1, q)
            dve.wait_ge(flag("searched"), 2 + N // P)
            panel(KNN, 0, NEAR, 3)
            with dve.Fori(1, PANELS) as p:
                panel(KNN, p, KNN, p - 1)
            for s in range(GCN1, NORMED + 1):
                panel(s, 0, s - 1, 3)
                with dve.Fori(1, PANELS) as p:
                    panel(s, p, s, p - 1)
            for q in range(PIECES):
                finish(NORMED, 3, q)

        @block.tensor
        def _(pe):
            mm = pe.matmul

            def chunk(t, i):
                return t[:, i * BANK:(i + 1) * BANK]

            def by_weights(name, src, weights):
                for i in range(CH):
                    last = mm(chunk(e0, i), weights[:, :], chunk(src, i), start=True, stop=True)
                last.then_inc(flag(name), 1)

            def by_tiles(name, dst, src, right):
                for k in range(KT):
                    last = mm(dst[:, k * D:(k + 1) * D], src[:, k * P:(k + 1) * P], right[:, :], start=True, stop=True)
                last.then_inc(flag(name), 1)

            def turned(name, dst, src):
                for k in range(KT):
                    last = pe.transpose(dst[:, k * D:(k + 1) * D], src[:, k * P:(k + 1) * P], ident[:, :])
                last.then_inc(flag(name), 1)

            def sums_down(name, col, *srcs):
                for k in range(KT):
                    for i, src in enumerate(srcs):
                        last = mm(ps[:, col + k:col + k + 1], src[:, k * P:(k + 1) * P], ones[:, 0:1],
                                  start=i == 0, stop=i == len(srcs) - 1)
                last.then_inc(flag(name), 1)

            def add_turned(name, p, src):
                for k in range(KT):
                    last = mm(acc(p, k * P, P), src[:, k * P:(k + 1) * P], ident[:, :], start=False,
                              stop=k % (BANK // P) == BANK // P - 1)
                last.then_inc(flag(name), 1)

            def weigh(q, a, first=False, last=False):
                for j in range(JT):
                    at_col = 2 * (JT * piece_at(HYPER, q) + j)
                    factors = g_parts[:, at_col:at_col + P]
                    for i in range(CH):
                        mm(chunk(e1, i), factors, chunk(a[:, j], i), start=first and j == 0,
                           stop=last and j == JT - 1)

            def product(s, p, q):
                b, slot, stays = BUF[s], slot_of(s, q), s in (KNN, NORMED)
                if q == 0:
                    pe.wait_ge(acc_free, evictions(s, p) - 2)
                if q % 4 == 0 and isinstance(p, int):
                    pe.wait_ge(x_ready[s], q // 4 + 1)
                at_tile = JT * piece_at(s, q)
                if not kept(s, p, q):
                    pe.wait_ge(hi_ready, hi_count(s, p, q))
                for j in range(JT):
                    for x_part in (xh[b], xl[b]):
                        for i in range(CH):
                            mm(acc(p, i * BANK, BANK), x_part[:, at_tile + j, :], chunk(high[:, q % HI, j], i),
                               start=(q, j) == (0, 0) and x_part is xh[b], stop=False)
                if s == HYPER and q in g_pe(p):
                    if q == g_pe(p)[0]:
                        pe.wait_ge(flag("g_padded"), 1)
                        pe.wait_ge(flag("den_rows_up"), 1 + p)
                    weigh(q, high[:, q % HI], first=q == g_pe(p)[0])
                if not kept(s, p, q):
                    by_pool, count = low_count(s, p, q)
                    pe.wait_ge(lo_pool if by_pool else lo_dve, count)
                if s == HYPER and q in g_pe(p):
                    weigh(q, low[:, slot], last=q == g_pe(p)[-1])
                for j in range(JT):
                    for i in range(CH):
                        last = mm(acc(p, i * BANK, BANK), xh[b][:, at_tile + j, :], chunk(low[:, slot, j], i),
                                  start=False, stop=(q, j) == (PIECES - 1, JT - 1) and not stays)
                last.then_inc(raw_free, 1)

            def product_early(m):
                n, p, q = SMOOTHED[m]
                if n == SUMMED + LATE.index((0, 0)):
                    pe.wait_ge(acc_free, 2 + smooth_ended(2))
                pe.wait_ge(x_ready[SMOOTH], q // PER_X + 1)
                pe.wait_ge(hi_ready, m + 1)
                for j in range(JT):
                    for x_part in (xh[BUF[SMOOTH]], xl[BUF[SMOOTH]]):
                        for i in range(CH):
                            mm(acc(p, i * BANK, BANK, SMOOTH), x_part[:, JT * q + j, :], chunk(high[:, m % HI, j], i),
                               start=(q, j) == (0, 0) and x_part is xh[BUF[SMOOTH]], stop=False)
                pe.wait_ge(lo_pool if POOL_FIRST[m] else lo_dve, POOL_FIRST[:m + 1].count(POOL_FIRST[m]))
                for j in range(JT):
                    for i in range(CH):
                        last = mm(acc(p, i * BANK, BANK, SMOOTH), xh[BUF[SMOOTH]][:, JT * q + j, :],
                                  chunk(low[:, n % RAW, j], i), start=False, stop=(q, j) == (PIECES - 1, JT - 1))
                last.then_inc(raw_free, 1)

            def finish(s, p, q):
                if s == SUMS:
                    if q == 4:
                        pe.wait_ge(flag("sums_diag"), p + 1)
                        for i in range(CH):
                            last = mm(chunk(e1, i), ones[:, :], chunk(xr, i), start=True, stop=True)
                        last.then_inc(flag("sums_d_bc"), 1)
                        pe.wait_ge(flag("sums_d_bc"), p + 1)
                        pe.sem_inc(xr_used, 1)
                if s == SMOOTH:
                    if q == 3:
                        pe.wait_ge(acc_free, 2 + smooth_ended(p))
                        by_weights("smooth_w", t0, w["w01"])
                    if q == 9:
                        pe.wait_ge(flag("z_square"), smooth_ended(p))
                        for i in range(CH):
                            mm(chunk(e1, i), neg_half[:, :], chunk(t2, i), start=True, stop=True)
                        sums_down("z_norms", E0, t2)
                if s == KNN:
                    if q == 4:
                        pe.wait_ge(flag("picked"), p + 1)
                        add_turned("knn_acc", p, t2)
                    if q == 6:
                        pe.wait_ge(acc_free, evictions(s, p))
                        by_tiles("knn_rows", e0, t0, w["w02"])
                if s == GCN1:
                    if q == 3:
                        pe.wait_ge(acc_free, evictions(s, p))
                        by_weights("gcn1_w", t0, w["w11"])
                    if q == 7:
                        pe.wait_ge(flag("gcn1_h"), p + 1)
                        by_tiles("gcn1_rows", e1, t1, w["w12"])
                if s == GCN2:
                    if q == 2:
                        pe.wait_ge(acc_free, evictions(s, p))
                        turned("gcn2_rows", e0, t0)
                    if q == 6:
                        pe.wait_ge(flag(f"y_up{s}"), p + 1)
                        turned("gcn2_xt", e0, t2)
                    if q == 8:
                        pe.wait_ge(flag("gcn2_xt_read"), p + 1)
                        by_tiles("gcn2_mx", e0, t0, w["w2"])
                if s == HYPER:
                    if q == 2:
                        pe.wait_ge(acc_free, evictions(s, p))
                        turned("hyper_rows", e0, t0)
                        pe.wait_ge(flag("g_whole_up"), 1 + p + 1)
                        pe.wait_ge(flag("den_rows_up"), 1 + p + 1)
                        for k in range(KT):
                            mm(acc(p, k, 1), g_whole[:, k * P:(k + 1) * P], ones[:, 0:1], start=True, stop=False)
                            last = mm(acc(p, k, 1), t1[:, k * P:(k + 1) * P], pick[:, :], start=False, stop=True)
                        last.then_inc(flag("hyper_den"), 1)
                    if q == 6:
                        pe.wait_ge(flag("hyper_norm"), p + 1)
                if s == NORMED:
                    if q == 2:
                        pe.wait_ge(flag("normed_sx"), p + 1)
                        add_turned("normed_acc", p, t1)
                    if q == 6:
                        pe.wait_ge(acc_free, evictions(s, p))
                        by_tiles("normed_rows", e0, t0, w["w3"])

            def panel(s, p, done, dp):
                for q in range(PIECES):
                    for step in ends_with(s, done, q):
                        finish(done, dp, step)
                    product(s, p, q)

            def read_sums(p):
                pe.wait_ge(flag("sums_steps"), PIECES * (p + 1))
                if p > 0:
                    pe.wait_ge(flag("d_bc_up"), p)
                sums_down("sums_read", E1, a_sum[:, p % 2, 0], a_sum[:, p % 2, 1])

            for p in range(PANELS):
                for t in range(PIECES):
                    if p > 0 and t == PIECES - PER_X:
                        read_sums(p)
                    n = PIECES * p + t
                    if n in STREAMED_AS:
                        product_early(STREAMED_AS[n])
                    else:
                        pe.wait_ge(flag("sums_steps"), n + 1)
                        pe.wait_ge(raw_free, RAW + n)
                        pe.sem_inc(raw_free, 1)
                if p == 0:
                    pe.wait_ge(consts_in, 16 * 10)
                    pe.wait_ge(consts_up, 6)
                    read_sums(0)
                if p < PANELS - 1:
                    finish(SUMS, p, 4)
            for i, ends in enumerate(LATE_ENDS):
                for end in ends:
                    finish(*end)
                product_early(len(EARLY) + i)
            for q in range(PIECES):
                finish(SMOOTH, 0, q)

            pe.wait_ge(flag("h_up"), PANELS)
            pe.wait_ge(flag("z_low"), PANELS)
            pe.wait_ge(flag("sq_col_up"), PANELS)
            with pe.Fori(0, PANELS) as p:
                for k in range(KT):
                    pe.wait_ge(flag("staged"), 2 * (KT * p + k + 1))
                    for i in range(8):
                        if i % CH == 0:
                            pe.wait_ge(flag("scores_out"), 4 * (KT * p + k) + i // CH + 1)
                        dst = chunk(ps, i)
                        mm(dst, z_tile_h[k % 2][:, :], chunk(zh, i), start=True, stop=False)
                        mm(dst, z_tile_h[k % 2][:, :], chunk(zl, i), start=False, stop=False)
                        last = mm(dst, z_tile_l[k % 2][:, :], chunk(zh, i), start=False, stop=False)
                        if i == 7:
                            last.then_inc(flag("staging_free"), 1)
                        last = mm(dst, ones_r[:, :], chunk(h_rows, i), start=False, stop=True)
                        if i % CH == CH - 1:
                            last.then_inc(flag("scores_up"), 1)

            pe.wait_ge(flag("scores_out"), 4 + 4 * N // P)
            panel(KNN, 0, NEAR, 3)
            with pe.Fori(1, PANELS) as p:
                panel(KNN, p, KNN, p - 1)
            for s in range(GCN1, NORMED + 1):
                panel(s, 0, s - 1, 3)
                with pe.Fori(1, PANELS) as p:
                    panel(s, p, s, p - 1)
            for q in range(PIECES):
                finish(NORMED, 3, q)


def kernel(**inputs):
    import numpy as np
    import concourse.bacc as bacc
    from concourse.bass_utils import run_bass_kernel_spmd as run

    nc = bacc.Bacc("TRN2", target_bir_lowering=False, num_devices=1)
    at = np.ascontiguousarray(np.asarray(inputs["adj"]).T.reshape(PIECES, JT, P, PANELS, PW).transpose(3, 0, 2, 1, 4))
    x = np.ascontiguousarray(np.asarray(inputs["x"]).reshape(PANELS, KT, P, D).transpose(0, 2, 1, 3)
                             .reshape(PANELS, P, KT * D))
    arrays = {"at": at, "x_in": x}
    for short, name in (("w01", "L0_gnn_W1"), ("b01", "L0_gnn_b1"), ("w02", "L0_gnn_W2"), ("b02", "L0_gnn_b2"),
                        ("w11", "L1_gnn_W1"), ("b11", "L1_gnn_b1"), ("w12", "L1_gnn_W2"), ("b12", "L1_gnn_b2"),
                        ("w2", "L2_gnn_W"), ("w3", "L3_gnn_weight")):
        arrays[short] = np.ascontiguousarray(np.asarray(inputs[name]))
    args = [nc.dram_tensor(n, a.shape, mybir.dt.from_np(a.dtype), kind="ExternalInput").ap() for n, a in arrays.items()]
    out = nc.dram_tensor("out", [PANELS, P, KT * D], F32, kind="ExternalOutput").ap()
    build(nc, *args, out)
    r = run(nc, [arrays], core_ids=[0])
    got = np.asarray(r.results[0]["out"]).reshape(PANELS, P, KT, D).transpose(0, 2, 1, 3)
    return np.ascontiguousarray(got.reshape(N, D))
```
